# Optimizing a Trainium2 kernel written in Bass

```python
import numpy as np
import jax
import jax.numpy as jnp

def _softmax(x, axis=-1):
    return jax.nn.softmax(x, axis=axis)

def _gelu(x):
    return jax.nn.gelu(x, approximate=True)

def _silu(x):
    return jax.nn.silu(x)

def _sigmoid(x):
    return jax.nn.sigmoid(x)

def _layernorm(x, axis=-1, eps=1e-05):
    m = jnp.mean(x, axis=axis, keepdims=True)
    v = jnp.var(x, axis=axis, keepdims=True)
    return (x - m) / jnp.sqrt(v + eps)

def _scatter_add(tgt, idx, src, axis=0):
    return tgt.at[idx].add(src)

def _segment_sum(src, seg, n):
    return jax.ops.segment_sum(src, seg, n)
kernel_name = 'mk_seq_postln_d1_jaxref_r4_9fa705'

def setup_inputs(seed: int=0):
    np.random.seed(seed)
    _w = jnp.asarray

    def _L0_attn_setup():
        import jax, jax.numpy as jnp
        import numpy as np
        B, N, C = (32, 128, 256)
        H = 16
        D = C // H
        MAX_SEQ = 128
        BASE = 10000.0

        def _rope_tables(n, d):
            position = jnp.arange(n, dtype=jnp.float32)[:, None]
            div_term = jnp.exp(jnp.arange(0, d, 2, dtype=jnp.float32) * (-np.log(BASE) / d))
            ang = position * div_term
            return (jnp.sin(ang), jnp.cos(ang))

        def _apply_rope(x, sin, cos):
            x1 = x[..., ::2]
            x2 = x[..., 1::2]
            out = jnp.stack([x1 * cos - x2 * sin, x1 * sin + x2 * cos], axis=-1)
            return out.reshape(*x.shape[:-1], -1)
        key = jax.random.key(seed)
        k1, k2, k3, k4, k5 = jax.random.split(key, 5)
        s = 0.02
        return {'x': jax.random.normal(k1, (B, N, C), dtype=jnp.float32), 'w_qkv': jax.random.normal(k2, (3 * C, C), dtype=jnp.float32) * s, 'b_qkv': jax.random.normal(k3, (3 * C,), dtype=jnp.float32) * s, 'w_lepe': jax.random.normal(k4, (C, 1, 3), dtype=jnp.float32) * s, 'b_lepe': jax.random.normal(k5, (C,), dtype=jnp.float32) * s}
    _L0_attn_in = _L0_attn_setup()

    def _L0_ffn_setup():
        import jax, jax.numpy as jnp
        import numpy as np
        import math
        D_IN = 256
        FEATURES = (1024, 1024, 256)
        BATCH, SEQ = (8, 512)

        def _conn_dense(kernel_bool, x):
            w = jnp.where(kernel_bool, jnp.float32(1.0), jnp.float32(-1.0))
            return x @ w
        key = jax.random.key(seed)
        kx, kk0, kk1, kk2 = jax.random.split(key, 4)
        x = jax.random.normal(kx, (BATCH, SEQ, D_IN), dtype=jnp.float32)
        k0 = jax.random.randint(kk0, (2 * D_IN, FEATURES[0]), 0, 2).astype(jnp.bool_)
        k1 = jax.random.randint(kk1, (FEATURES[0], FEATURES[1]), 0, 2).astype(jnp.bool_)
        k2 = jax.random.randint(kk2, (FEATURES[1], FEATURES[2]), 0, 2).astype(jnp.bool_)
        s0 = jnp.asarray(1.0 / math.sqrt(2 * D_IN), dtype=jnp.float32)
        s1 = jnp.asarray(1.0 / math.sqrt(FEATURES[0]), dtype=jnp.float32)
        s2 = jnp.asarray(1.0 / math.sqrt(FEATURES[1]), dtype=jnp.float32)
        return {'x': x, 'k0': k0, 'k1': k1, 'k2': k2, 's0': s0, 's1': s1, 's2': s2}
    _L0_ffn_in = _L0_ffn_setup()
    _d = {'L0_attn_x': _L0_attn_in['x'], 'L0_attn_w_qkv': _L0_attn_in['w_qkv'], 'L0_attn_b_qkv': _L0_attn_in['b_qkv'], 'L0_attn_w_lepe': _L0_attn_in['w_lepe'], 'L0_attn_b_lepe': _L0_attn_in['b_lepe'], 'L0_ffn_k0': _L0_ffn_in['k0'], 'L0_ffn_k1': _L0_ffn_in['k1'], 'L0_ffn_k2': _L0_ffn_in['k2'], 'L0_ffn_s0': _L0_ffn_in['s0'], 'L0_ffn_s1': _L0_ffn_in['s1'], 'L0_ffn_s2': _L0_ffn_in['s2']}
    _x0 = _d['L0_attn_x']
    _d['L0_attn_x'] = jax.random.normal(jax.random.fold_in(jax.random.key(seed), 1), (8, 1024, 256), dtype=_x0.dtype)
    del _x0
    return _d

def reference(L0_attn_x, L0_attn_w_qkv, L0_attn_b_qkv, L0_attn_w_lepe, L0_attn_b_lepe, L0_ffn_k0, L0_ffn_k1, L0_ffn_k2, L0_ffn_s0, L0_ffn_s1, L0_ffn_s2):

    def _L0_attn_ref(x, w_qkv, b_qkv, w_lepe, b_lepe):
        import jax, jax.numpy as jnp
        import numpy as np
        B, N, C = (32, 128, 256)
        H = 16
        D = C // H
        MAX_SEQ = 128
        BASE = 10000.0

        def _rope_tables(n, d):
            position = jnp.arange(n, dtype=jnp.float32)[:, None]
            div_term = jnp.exp(jnp.arange(0, d, 2, dtype=jnp.float32) * (-np.log(BASE) / d))
            ang = position * div_term
            return (jnp.sin(ang), jnp.cos(ang))

        def _apply_rope(x, sin, cos):
            x1 = x[..., ::2]
            x2 = x[..., 1::2]
            out = jnp.stack([x1 * cos - x2 * sin, x1 * sin + x2 * cos], axis=-1)
            return out.reshape(*x.shape[:-1], -1)
        b, n, c = x.shape
        scale = 1.0 / np.sqrt(D)
        sin, cos = _rope_tables(n, D)
        qkv = (x @ w_qkv.T + b_qkv).reshape(b, n, 3, H, D).transpose(2, 0, 3, 1, 4)
        q, k, v = (qkv[0], qkv[1], qkv[2])
        q = jax.nn.elu(q) + 1.0
        k = jax.nn.elu(k) + 1.0
        q = _apply_rope(q, sin, cos)
        k = _apply_rope(k, sin, cos)
        attn = jnp.einsum('bhnd,bhmd->bhnm', q, k) * scale
        attn = jax.nn.softmax(attn, axis=-1)
        attn_out = jnp.einsum('bhnm,bhmd->bhnd', attn, v)
        attn_out = attn_out.transpose(0, 2, 1, 3).reshape(b, n, c)
        v_conv = v.transpose(0, 2, 1, 3).reshape(b, n, c).transpose(0, 2, 1)
        lepe = jax.lax.conv_general_dilated(v_conv, w_lepe, window_strides=(1,), padding=((1, 1),), dimension_numbers=('NCH', 'OIH', 'NCH'), feature_group_count=c) + b_lepe[None, :, None]
        lepe = lepe.transpose(0, 2, 1)
        return attn_out + lepe

    def _L0_ffn_ref(x, k0, k1, k2, s0, s1, s2):
        import jax, jax.numpy as jnp
        import numpy as np
        import math
        D_IN = 256
        FEATURES = (1024, 1024, 256)
        BATCH, SEQ = (8, 512)

        def _conn_dense(kernel_bool, x):
            w = jnp.where(kernel_bool, jnp.float32(1.0), jnp.float32(-1.0))
            return x @ w
        h = jnp.concatenate([x, -x], axis=-1)
        h = s0 * _conn_dense(k0, h)
        h = jax.nn.relu(h) * 2
        h = s1 * _conn_dense(k1, h)
        h = jax.nn.relu(h) * 2
        h = s2 * _conn_dense(k2, h)
        return h
    x = L0_attn_x
    x = _layernorm(x + _L0_attn_ref(x, L0_attn_w_qkv, L0_attn_b_qkv, L0_attn_w_lepe, L0_attn_b_lepe), axis=-1)
    x = _layernorm(x + _L0_ffn_ref(x, L0_ffn_k0, L0_ffn_k1, L0_ffn_k2, L0_ffn_s0, L0_ffn_s1, L0_ffn_s2), axis=-1)
    return x

_drawn_inputs = setup_inputs


def setup_inputs(seed=0):
    import zlib

    import numpy as np

    out = dict(_drawn_inputs(seed))
    spreads = {}
    factors = {'L0_attn_w_qkv': 2.776, 'L0_attn_w_lepe': 5.141, 'L0_attn_b_lepe': 2.97}
    for name, (base, spread) in spreads.items():
        noise = np.random.default_rng([zlib.crc32(name.encode()), seed]).standard_normal(out[name].shape)
        drawn = base * np.exp(spread * noise) if base else spread * noise
        out[name] = jnp.asarray(drawn.astype(out[name].dtype))
    for name, factor in factors.items():
        out[name] = (out[name] * factor).astype(out[name].dtype)
    return out
```

```python
from contextlib import ExitStack

import numpy as np
import concourse.bass as bass
from concourse import mybir

ALU = mybir.AluOpType
ACT = mybir.ActivationFunctionType
AXIS_X = mybir.AxisListType.X
F32 = mybir.dt.float32
BF16 = mybir.dt.bfloat16
F16 = mybir.dt.float16
U8 = mybir.dt.uint8

P = 128
NB, N, C = 8, 1024, 256
H, D = 16, 16
F = 1024
T = N // P
KC = C // P
KF = F // P
PAIRS = H // 2
RING = 4
LEAD = 3
PARTS = 3
STACK = 6 * D
Q_PART = (0, 0, 0, 1, 1, 2)
K_PART = (0, 1, 2, 0, 1, 0)
EPS = 1e-5
H_SCALE = 2.0 ** 11
Y0_SCALE = 2.0 ** 6
Y1_SCALE = 2.0 ** -4
HI_PER_BATCH = 2 + 4 * T // 2
SPLIT_OPS = 14
LEPE_OPS = 7
MAX_OPS = 4
LN_OPS = 2 * T
LOAD = 16 * 9

PROJ = ("qA", "qB", "kA", "kB")


def b_units(ffn, proj):
    l0 = lambda th: [("L0", th, u) for u in range(4)]
    l1 = lambda th: [("L1", th, u) for u in range(4)]
    order = [("proj", 0), ("proj", 1), ("hT", 0), ("hT", 1), *l0(0), *l1(0), ("proj", 2), ("proj", 3),
             *l0(1), ("L2", 0), *l1(1), ("V", 0), ("V", 1), ("L2", 1)]
    return [u for u in order if (proj if u[0] in ("proj", "V") else ffn)]


def plan_units(kind):
    units, bank = [], []
    if kind == "start":
        units += b_units(False, True)
        units += [("S", -1, v, h) for v in range(T + LEAD) for h in range(2)]
        return units, [("max rows", -1)]
    if kind == "end":
        return b_units(True, False), [("O rows", -1)]
    if kind != "first":
        bank.append(("O rows", -1))
    for j in range(PAIRS):
        if j == PAIRS // 2:
            units += b_units(kind != "first", kind != "last")
            bank.append(("O rows", j - 1))
        elif j > 0:
            bank.append(("O rows", j - 1))
        for kt in range(T):
            for h in range(2):
                if has_scores(kind, j, kt):
                    units.append(("S", j, kt, h))
                units.append(("T", j, kt, h))
        if kind != "last" or j < PAIRS - 1:
            bank.append(("max rows", j))
    return units, bank


def has_scores(kind, j, kt):
    return kind != "last" or (j + 1) * T + kt + LEAD < PAIRS * T


class Units:

    def __init__(self, full, free):
        self.full, self.free = full, free
        self.at, self.total = {}, {}
        for kind in ("start", "first", "mid", "last", "end"):
            units, bank = plan_units(kind)
            used = [0, 0, 0, 0]
            for n, u in enumerate(units):
                self.at[kind, u] = (n % 3, used[n % 3])
                used[n % 3] += 1
            for u in bank:
                self.at[kind, u] = (3, used[3])
                used[3] += 1
            self.total[kind] = used

    def place(self, kind, unit):
        return self.at[kind, unit][0]

    def uses(self, kind, b, unit):
        p, n = self.at[kind, unit]
        return self.count(kind, b, p, n)

    def count(self, kind, b, p, n):
        t = self.total
        if kind == "start":
            return n
        n += t["start"][p]
        if kind == "first":
            return n
        n += t["first"][p]
        if kind == "mid":
            return b * t["mid"][p] + (n - t["mid"][p])
        n += (NB - 2) * t["mid"][p]
        return n if kind == "last" else n + t["last"][p]

    def wait_all_read(self, eng, kind, b):
        for p in range(3):
            wait(eng, self.free[p], self.count(kind, b, p, 0))

    def wait_free(self, eng, kind, b, unit):
        wait(eng, self.free[self.place(kind, unit)], self.uses(kind, b, unit))

    def wait_free_and_read(self, eng, kind, b, unit, source):
        if self.place(kind, source) == self.place(kind, unit):
            assert self.at[kind, unit][1] > self.at[kind, source][1]
        else:
            self.wait_read(eng, kind, b, source)
        self.wait_free(eng, kind, b, unit)

    def wait_full(self, eng, kind, b, unit):
        wait(eng, self.full[self.place(kind, unit)], self.uses(kind, b, unit) + 1)

    def wait_read(self, eng, kind, b, unit):
        wait(eng, self.free[self.place(kind, unit)], self.uses(kind, b, unit) + 1)


def wait(eng, sem, value):
    if isinstance(value, int) and value <= 0:
        return
    eng.wait_ge(sem, value)


def wait_apart(eng, sem, value, long_over):
    if not isinstance(value, int):
        value = eng.to_reg(value)
    eng.wait_ge(*long_over)
    eng.wait_ge(sem, value)


def over_batches(eng, iteration):
    iteration("first", 0)
    with eng.Fori(1, NB - 1) as b:
        iteration("mid", b)
    iteration("last", NB - 1)


def build(nc, x, xT, wT, b_qk, b_v, w_lepe, b_lepe, cos, sin, k0, k1, k2, s0, s1, s2, out):
    with ExitStack() as ctx:
        def sb(name, shape, dt):
            return ctx.enter_context(nc.sbuf_tensor(name, shape, dt))

        def sem(name):
            return ctx.enter_context(nc.semaphore(name))

        q_scratch = nc.dram_tensor("q_scratch", [NB, PARTS, 2, P, N], BF16)
        k_scratch = nc.dram_tensor("k_scratch", [NB, PARTS, 2, P, N], BF16)

        q_stack = sb("q_stack", [P, RING, 2 * N], BF16)
        k_stack = sb("k_stack", [P, RING, 2 * N], BF16)
        v_pair = sb("v_pair", [P, RING, T, 2, 32], F32)
        v_ext = sb("v_ext", [P, T + 2, C], F32)
        xT_sb = sb("xT_sb", [P, KC, N], F32)
        base = sb("base", [P, T, C], F32)
        attn = sb("attn", [P, T, C], F32)
        hres = sb("hres", [P, T, C], F32)
        probs = sb("probs", [P, 4, N], F32)
        wT_sb = sb("wT_sb", [P, KC, 3 * C], F32)
        w0 = sb("w0", [P, KC, F], F16)
        w1 = sb("w1", [P, KF, F], F16)
        w2 = sb("w2", [P, KF, C], F16)
        rope = sb("rope", [P, 2, N], F32)
        cos_sb, sin_sb = rope[:, 0], rope[:, 1]
        work = sb("work", [P, 4, N], F32)
        parts = sb("parts", [P, PARTS, N], BF16)
        hT = sb("hT", [P, 2, KC, N], F16)
        h0T = sb("h0T", [P, 2, KF, N // 2], F16)
        h1T = sb("h1T", [P, 2, KF, N // 2], F16)
        o_sb = sb("o_sb", [P, 512], F32)
        lepe_rows = sb("lepe_rows", [P, 5, C], F32)
        ident = sb("ident", [P, P], F32)
        ident16 = sb("ident16", [P, P], BF16)
        bias_qk = sb("bias_qk", [P, 4], F32)
        maxima = sb("maxima", [P, 2, 2 * T], F32)
        max_rest = sb("max_rest", [P, 2 * T], F32)
        max_parts = sb("max_parts", [P, P], BF16)
        max_rows = sb("max_rows", [P, P], BF16)
        rden = sb("rden", [P, 2 * T], F32)
        stats = sb("stats", [P, T, 6], F32)
        moments = sb("moments", [P, T, 2], F32)
        var_eps = sb("var_eps", [P, T], F32)
        neg_mean = sb("neg_mean", [P, T], F32)
        ln_consts = sb("ln_consts", [P, T, 4], F32)
        rstd = sb("rstd", [P, T], F32)
        shift = sb("shift", [P, T], F32)
        s_in = sb("s_in", [P, 3], F32)
        s_sign = sb("s_sign", [P, 3], F32)
        s_work = sb("s_work", [P, 6], F32)
        out_scale = s_work[:, 5:6]
        stage0 = h0T[:].rearrange("p a k n -> p (a k n)").bitcast(U8)
        stage1 = h1T[:].rearrange("p a k n -> p (a k n)").bitcast(U8)
        k0_u8 = stage0[:, 0:2 * KC * F].rearrange("p (k n) -> p k n", n=F)
        k2_u8 = stage0[:, 2 * KC * F:2 * KC * F + KF * C].rearrange("p (k n) -> p k n", n=C)
        k1_u8 = stage1[:, 0:KF * F].rearrange("p (k n) -> p k n", n=F)

        slots = [ctx.enter_context(nc.psum_tensor(f"slot{i}", [P, N], F32)) for i in range(3)]
        o_bank = ctx.enter_context(nc.psum_tensor("o_bank", [P, 512], F32))
        t_bank = ctx.enter_context(nc.psum_tensor("t_bank", [P, 512], F32))

        unit_full = [sem(f"unit_full{i}") for i in range(4)]
        unit_free = [sem(f"unit_free{i}") for i in range(4)]
        weights_loaded = sem("weights_loaded")
        k_loaded = sem("k_loaded")
        xT_loaded = sem("xT_loaded")
        x_loaded = sem("x_loaded")
        stack_loaded = [sem(f"stack_loaded{i}") for i in range(RING)]
        max_loaded = sem("max_loaded")
        edges_loaded = sem("edges_loaded")
        scratch_written = sem("scratch_written")
        out_stored = sem("out_stored")
        pool_setup = sem("pool_setup")
        dve_setup = sem("dve_setup")
        weights_ready = sem("weights_ready")
        max_split = sem("max_split")
        pv_done = sem("pv_done")
        o_copied = sem("o_copied")
        v_copied = sem("v_copied")
        reciprocal_done = sem("reciprocal_done")
        attn_written = sem("attn_written")
        sum_ready = sem("sum_ready")
        lepe_done = sem("lepe_done")
        elu_done = sem("elu_done")
        split_done = sem("split_done")
        ln_stats = sem("ln_stats")
        ln_scale = sem("ln_scale")
        ln_done = sem("ln_done")
        hi_ready = sem("hi_ready")
        units = Units(unit_full, unit_free)

        block = ctx.enter_context(nc.Block())

        q_rows = q_scratch.ap().rearrange("b t c (i h) n -> b (t c i) (h n)", h=H)
        k_rows = k_scratch.ap().rearrange("b t c (i h) n -> b (t c i) (h n)", h=H)

        @block.sync
        def _(sp):
            def load_stacks(b, j):
                r = j % RING
                cols = slice(j * 2 * N, (j + 1) * 2 * N)
                for blk, part in enumerate(Q_PART):
                    sp.dma_start(q_stack[blk * D:(blk + 1) * D, r], q_rows[b, part * D:(part + 1) * D, cols])\
                      .then_inc(stack_loaded[r], 16)
                for blk, n in ((0, 3), (3, 2), (5, 1)):
                    sp.dma_start(k_stack[blk * D:(blk + n) * D, r], k_rows[b, 0:n * D, cols])\
                      .then_inc(stack_loaded[r], 16)

            def load_max(kind, b, j):
                units.wait_read(sp, kind, b, ("max rows", j))
                for p in range(PARTS):
                    sp.dma_start(q_stack[STACK + p:STACK + p + 1, (j + 1) % RING].rearrange("o (r q) -> o r q", q=P),
                                 max_rows[p * 2 * T:(p + 1) * 2 * T, :]).then_inc(max_loaded, 16)

            def load_x(b):
                sp.dma_start(base[:], x[b]).then_inc(x_loaded, 16)

            def load_edges(kind, b):
                units.wait_read(sp, kind, b, ("V", 1))
                sp.dma_start(v_ext[1:P, 0, :], v_ext[0:P - 1, T, :]).then_inc(edges_loaded, 16)
                sp.dma_start(v_ext[0:P - 1, T + 1, :], v_ext[1:P, 1, :]).then_inc(edges_loaded, 16)

            def store_out(m):
                sp.wait_ge(ln_done, (m * 2 + 2) * T)
                sp.dma_start(out[m], hres[:]).then_inc(out_stored, 16)

            sp.dma_start(xT_sb[:], xT[0]).then_inc(xT_loaded, 16)
            sp.dma_start(wT_sb[:], wT).then_inc(weights_loaded, 16)
            sp.dma_start(bias_qk[:], b_qk).then_inc(weights_loaded, 16)
            sp.dma_start(rope[:, 0], cos).then_inc(weights_loaded, 16)
            sp.dma_start(rope[:, 1], sin).then_inc(weights_loaded, 16)
            for i in range(3):
                sp.dma_start(lepe_rows[:, i], w_lepe[i].partition_broadcast(P)).then_inc(weights_loaded, 16)
            sp.dma_start(lepe_rows[:, 3], b_lepe.partition_broadcast(P)).then_inc(weights_loaded, 16)
            sp.dma_start(lepe_rows[:, 4], b_v.partition_broadcast(P)).then_inc(weights_loaded, 16)
            load_x(0)
            for i, s in enumerate((s0, s1, s2)):
                sp.dma_start(s_in[:, i:i + 1], s.partition_broadcast(P)).then_inc(k_loaded, 16)
            sp.dma_start(k0_u8, k0.rearrange("(k p) n -> p k n", p=P)).then_inc(k_loaded, 16)
            sp.dma_start(k1_u8, k1.rearrange("(k p) n -> p k n", p=P)).then_inc(k_loaded, 16)
            sp.dma_start(k2_u8, k2.rearrange("(k p) n -> p k n", p=P)).then_inc(k_loaded, 16)
            units.wait_full(sp, "start", 0, ("V", 1))
            sp.dma_start(xT_sb[:], xT[1]).then_inc(xT_loaded, 16)
            load_edges("start", 0)
            sp.wait_ge(scratch_written, 4 * 16)
            for j in range(RING):
                load_stacks(0, j)
            load_max("start", 0, -1)

            def iteration(kind, b):
                for j in range(PAIRS):
                    if j == PAIRS // 2 and kind != "last":
                        load_edges(kind, b)
                        if kind == "first":
                            units.wait_full(sp, kind, b, ("V", 1))
                            sp.dma_start(xT_sb[:], xT[2]).then_inc(xT_loaded, 16)
                        else:
                            units.wait_full(sp, kind, b, ("V", 1))
                            sp.dma_start(xT_sb[:], xT[b + 2]).then_inc(xT_loaded, 16)
                    if kind != "last" or j < PAIRS - 1:
                        load_max(kind, b, j)
                    if j == 0 and kind != "first":
                        sp.wait_ge(sum_ready, b)
                        load_x(b)
                    if j == 6 and kind != "first":
                        store_out(b - 1)
                    if kind == "last" and j + RING >= PAIRS:
                        continue
                    units.wait_full(sp, kind, b, ("T", j, T - 1, 1))
                    if j + RING < PAIRS:
                        load_stacks(b, j + RING)
                    else:
                        sp.wait_ge(scratch_written, b * 64 + 128)
                        load_stacks(b + 1, j + RING - PAIRS)

            over_batches(sp, iteration)
            store_out(NB - 1)
            sp.wait_ge(out_stored, 16 * (NB + 1))

        @block.tensor
        def _(pe):
            def slot_of(kind, unit):
                return slots[units.place(kind, unit)]

            def scores(kind, b, unit, j, t, h):
                s, r = slot_of(kind, unit), j % RING
                units.wait_free(pe, kind, b, unit)
                for half in range(2):
                    last = nc.tensor.matmul(s[:, half * 512:(half + 1) * 512],
                                            q_stack[0:STACK, r, h * N + t * P:h * N + (t + 1) * P],
                                            k_stack[0:STACK, r, h * N + half * 512:h * N + (half + 1) * 512],
                                            start=True, stop=True)
                last.then_inc(unit_full[units.place(kind, unit)], 1)

            def scores_T(kind, b, unit, j, kt, h):
                s, r = slot_of(kind, unit), j % RING
                rows = STACK + PARTS
                units.wait_free(pe, kind, b, unit)
                for half in range(2):
                    last = nc.tensor.matmul(s[:, half * 512:(half + 1) * 512],
                                            k_stack[0:rows, r, h * N + kt * P:h * N + (kt + 1) * P],
                                            q_stack[0:rows, r, h * N + half * 512:h * N + (half + 1) * 512],
                                            start=True, stop=True)
                last.then_inc(unit_full[units.place(kind, unit)], 1)

            def weighted_v(kind, b, j, kt):
                units.wait_read(pe, kind, b, ("T", j, kt, 1))
                if kt == 0:
                    wait(pe, v_copied, b * PAIRS + (j + 1))
                    wait(pe, o_copied, b * PAIRS + j)
                for half in range(2):
                    for h in range(2):
                        g = 2 * half + h
                        p = probs[:, 2 * (kt % 2) + h].rearrange("p (b f q) -> p b f q", f=2, q=P)
                        last = nc.tensor.matmul(o_bank[32 * g:32 * g + 32, :].rearrange("p (b q) -> p b q", q=P),
                                                v_pair[:, j % RING, kt, h, :], p[:, :, half, :],
                                                start=kt == 0, stop=kt == T - 1)
                last.then_inc(pv_done, 1)

            def max_rows_T(kind, b, j):
                unit = ("max rows", j)
                wait(pe, max_split, b * (PAIRS * MAX_OPS) + (j + 2) * MAX_OPS)
                units.wait_free(pe, kind, b, unit)
                nc.tensor.transpose(t_bank[:].bitcast(BF16)[:, 0:P], max_parts[:], ident16[:])\
                  .then_inc(unit_full[3], 1)

            def o_rows(kind, b, j):
                unit = ("O rows", j)
                pe.wait_ge(o_copied, b * PAIRS + (j + 1))
                units.wait_free(pe, kind, b, unit)
                for blk in range(4):
                    last = nc.tensor.transpose(t_bank[:, blk * P:(blk + 1) * P],
                                               o_sb[:, blk * P:(blk + 1) * P], ident[:])
                last.then_inc(unit_full[3], 1)

            def project(kind, b, ct):
                unit = ("proj", ct)
                s = slot_of(kind, unit)
                units.wait_free(pe, kind, b, unit)
                for half in range(2):
                    for kc in range(KC):
                        last = nc.tensor.matmul(s[:, half * 512:(half + 1) * 512],
                                                wT_sb[:, kc, ct * P:(ct + 1) * P],
                                                xT_sb[:, kc, half * 512:(half + 1) * 512],
                                                start=kc == 0, stop=kc == KC - 1)
                last.then_inc(unit_full[units.place(kind, unit)], 1)

            def project_v(kind, b, half):
                unit = ("V", half)
                s = slot_of(kind, unit)
                units.wait_free(pe, kind, b, unit)
                for t in range(4):
                    for kc in range(KC):
                        col = (4 * half + t) * P
                        last = nc.tensor.matmul(s[:, t * C:(t + 1) * C], xT_sb[:, kc, col:col + P],
                                                wT_sb[:, kc, 2 * C:3 * C], start=kc == 0, stop=kc == KC - 1)
                last.then_inc(unit_full[units.place(kind, unit)], 1)

            def transpose_h(kind, b, kc):
                unit = ("hT", kc)
                s = slot_of(kind, unit)
                units.wait_free(pe, kind, b, unit)
                for t in range(T):
                    last = nc.tensor.transpose(s[:, t * P:(t + 1) * P], hres[:, t, kc * P:(kc + 1) * P], ident[:])
                last.then_inc(unit_full[units.place(kind, unit)], 1)

            def hidden(kind, b, layer, th, u):
                unit = (layer, th, u)
                s = slot_of(kind, unit)
                tiles = KC if layer == "L0" else KF
                for k in range(tiles):
                    source = ("hT", 1) if layer == "L0" else ("L0", th, k // 2)
                    if k == 0:
                        units.wait_free_and_read(pe, kind, b, unit, source)
                    elif layer == "L1" and k % 2 == 0:
                        units.wait_read(pe, kind, b, source)
                    for i in range(2):
                        m = (2 * u + i) * P
                        for part in range(2):
                            if layer == "L0":
                                w, a = w0[:, k, m:m + P], hT[:, part, k, th * 512:(th + 1) * 512]
                            else:
                                w, a = w1[:, k, m:m + P], h0T[:, part, k, :]
                            last = nc.tensor.matmul(s[:, i * 512:(i + 1) * 512], w, a,
                                                    start=k == 0 and part == 0,
                                                    stop=k == tiles - 1 and part == 1)
                last.then_inc(unit_full[units.place(kind, unit)], 1)

            def ffn_out(kind, b, th):
                unit = ("L2", th)
                s = slot_of(kind, unit)
                units.wait_free_and_read(pe, kind, b, unit, ("L1", th, 3))
                for t in range(4):
                    for k in range(KF):
                        for part in range(2):
                            last = nc.tensor.matmul(s[:, t * C:(t + 1) * C], h1T[:, part, k, t * P:(t + 1) * P],
                                                    w2[:, k, :], start=k == 0 and part == 0,
                                                    stop=k == KF - 1 and part == 1)
                last.then_inc(unit_full[units.place(kind, unit)], 1)

            def stage_b(kind, b, after_unit):
                for n, unit in enumerate(b_units(kind not in ("start", "first"), kind not in ("last", "end"))):
                    if unit == ("hT", 0):
                        pe.wait_ge(ln_done, b * (2 * T) - T)
                    if unit == ("proj", 0):
                        pe.wait_ge(xT_loaded, b * 16 + 32 if kind != "start" else 16)
                    if unit[0] == "proj":
                        project(kind, b, unit[1])
                    elif unit[0] == "V":
                        project_v(kind, b, unit[1])
                    elif unit[0] == "hT":
                        transpose_h(kind, b, unit[1])
                    elif unit[0] == "L2":
                        ffn_out(kind, b, unit[1])
                    else:
                        hidden(kind, b, *unit)
                    if n in after_unit:
                        after_unit[n]()

            def stack_uses(b, j):
                return (b * (PAIRS // RING) + (j // RING + 1)) * LOAD

            pe.wait_ge(weights_loaded, 9 * 16)
            pe.wait_ge(pool_setup, 4)
            stage_b("start", 0, {})
            for v in range(T + LEAD):
                j = v // T
                if v % T == 0:
                    pe.wait_ge(stack_loaded[j], stack_uses(0, j))
                if v == 0:
                    pe.wait_ge(dve_setup, 2)
                for h in range(2):
                    scores("start", 0, ("S", -1, v, h), j, v % T, h)
            max_rows_T("start", 0, -1)

            def iteration(kind, b):
                for j in range(PAIRS):
                    if j == PAIRS // 2:
                        if kind == "first":
                            pass
                        stage_b(kind, b, {0: lambda: weighted_v(kind, b, j - 1, T - 1),
                                          1: lambda: o_rows(kind, b, j - 1)})
                    for kt in range(T):
                        ahead = j * T + kt + T + LEAD
                        if kt == 0:
                            pe.wait_ge(max_loaded, b * (PAIRS * 48) + (j + 1) * 48)
                        if ahead % T == 0 and has_scores(kind, j, kt):
                            n = ahead // T
                            pe.wait_ge(stack_loaded[n % RING], stack_uses(b, n))
                        for h in range(2):
                            if has_scores(kind, j, kt):
                                scores(kind, b, ("S", j, kt, h), ahead // T, ahead % T, h)
                            scores_T(kind, b, ("T", j, kt, h), j, kt, h)
                        if kt > 0:
                            weighted_v(kind, b, j, kt - 1)
                        elif j == 0 and kind != "first":
                            weighted_v_last_of_previous(kind, b)
                        elif j not in (0, PAIRS // 2):
                            weighted_v(kind, b, j - 1, T - 1)
                        if kt == 2 and j != PAIRS // 2 and not (j == 0 and kind == "first"):
                            o_rows(kind, b, j - 1)
                        if kt == 5 and (kind != "last" or j < PAIRS - 1):
                            max_rows_T(kind, b, j)

            def weighted_v_last_of_previous(kind, b):
                j, kt = PAIRS - 1, T - 1
                units.wait_all_read(pe, kind, b)
                for half in range(2):
                    for h in range(2):
                        g = 2 * half + h
                        p = probs[:, 2 * (kt % 2) + h].rearrange("p (b f q) -> p b f q", f=2, q=P)
                        last = nc.tensor.matmul(o_bank[32 * g:32 * g + 32, :].rearrange("p (b q) -> p b q", q=P),
                                                v_pair[:, j % RING, kt, h, :], p[:, :, half, :],
                                                start=False, stop=True)
                last.then_inc(pv_done, 1)

            over_batches(pe, iteration)
            weighted_v_last_of_previous("end", NB)
            o_rows("end", NB, -1)
            stage_b("end", NB, {})

        @block.scalar
        def _(act):
            def exp_probs(kind, b, j, kt, h):
                unit = ("T", j, kt, h)
                units.wait_full(act, kind, b, unit)
                if h == 0:
                    wait(act, pv_done, b * (PAIRS * T) + (j * T + kt - 1))
                place = units.place(kind, unit)
                nc.scalar.activation(probs[:, 2 * (kt % 2) + h], slots[place][:], ACT.Exp, scale=float(D) ** -0.5)\
                  .then_inc(unit_free[place], 1)

            def copy_o(kind, b, j):
                act.wait_ge(pv_done, b * (PAIRS * T) + (j + 1) * T)
                before = b * PAIRS + j
                if not (isinstance(before, int) and before == 0):
                    wait_o_rows(kind, b, j)
                nc.scalar.activation(o_sb[:], o_bank[:], ACT.Copy).then_inc(o_copied, 1)

            def wait_o_rows(kind, b, j):
                act.wait_ge(reciprocal_done, b * PAIRS + j)

            def copy_v(b, j):
                if not (isinstance(b, int) and b == 0 and j < RING):
                    act.wait_ge(pv_done, b * (PAIRS * T) + (j - RING + 1) * T)
                nc.scalar.activation(v_pair[:, j % RING, :, :, 0:D],
                                     v_ext[:, 1:T + 1, 2 * D * j:2 * D * (j + 1)]
                                     .rearrange("p t (h d) -> p t h d", d=D), ACT.Copy).then_inc(v_copied, 1)

            def tail(kind, b, j):
                copy_o(kind, b, j)
                n = j + RING
                if n < PAIRS:
                    copy_v(b, n)
                elif kind != "last":
                    if j == RING:
                        units.wait_read(act, kind, b, ("V", 1))
                    copy_v(b + 1, n - PAIRS)

            def elu_inputs(kind, b, ct):
                unit = ("proj", ct)
                units.wait_full(act, kind, b, unit)
                if ct % 2 == 0:
                    if kind != "start":
                        act.wait_ge(lepe_done, b * LEPE_OPS + LEPE_OPS)
                        act.wait_ge(split_done, b * (2 * SPLIT_OPS) + (2 + ct // 2) * SPLIT_OPS)
                    elif ct:
                        act.wait_ge(split_done, SPLIT_OPS)
                place = units.place(kind, unit)
                c = ct % 2
                nc.scalar.activation(work[:, 2 * c], slots[place][:], ACT.Exp, bias=bias_qk[:, ct:ct + 1])
                nc.scalar.activation(work[:, 2 * c + 1], slots[place][:], ACT.Relu, bias=bias_qk[:, ct:ct + 1])\
                  .then_inc(unit_free[place], 1)

            def high_part(kind, b, unit):
                units.wait_full(act, kind, b, unit)
                s = slots[units.place(kind, unit)]
                if unit[0] == "hT":
                    ins = nc.scalar.activation(hT[:, 0, unit[1], :], s[:], ACT.Copy, scale=H_SCALE)
                else:
                    u = unit[2]
                    dst = h0T if unit[0] == "L0" else h1T
                    ins = nc.scalar.activation(dst[:, 0, 2 * u:2 * u + 2, :],
                                               s[:].rearrange("p (i n) -> p i n", i=2), ACT.Relu)
                ins.then_inc(hi_ready, 1)

            def stage_b(kind, b, after_unit):
                for n, unit in enumerate(b_units(kind not in ("start", "first"), kind not in ("last", "end"))):
                    if unit[0] == "proj":
                        elu_inputs(kind, b, unit[1])
                    elif unit[0] in ("hT", "L0", "L1"):
                        high_part(kind, b, unit)
                    if n in after_unit:
                        after_unit[n]()

            def normalise(m2, which, t):
                if t == 0:
                    act.wait_ge(ln_scale, (m2 + which + 1) * 3)
                nc.scalar.activation(hres[:, t, :], hres[:, t, :], ACT.Identity, bias=shift[:, t:t + 1],
                                     scale=rstd[:, t:t + 1]).then_inc(ln_done, 1)

            act.wait_ge(weights_loaded, 9 * 16)
            stage_b("start", 0, {})
            act.wait_ge(pool_setup, 4)
            units.wait_read(act, "start", 0, ("V", 1))
            for j in range(RING):
                copy_v(0, j)

            def iteration(kind, b):
                for j in range(PAIRS):
                    if j == PAIRS // 2:
                        stage_b(kind, b, {0: lambda: tail(kind, b, j - 1)})
                    for kt in range(T):
                        for h in range(2):
                            exp_probs(kind, b, j, kt, h)
                        if kt == 0 and j == 0 and kind != "first":
                            tail_of_previous(kind, b)
                        elif kt == 0 and j not in (0, PAIRS // 2):
                            tail(kind, b, j - 1)
                        if j == 2 and kind != "first":
                            normalise(b * 2 - 2, 0, kt)
                        if j == 5 and kind != "first":
                            normalise(b * 2 - 2, 1, kt)

            def tail_of_previous(kind, b):
                copy_o(kind, b, -1)
                if kind != "end":
                    copy_v(b, RING - 1)

            over_batches(act, iteration)
            tail_of_previous("end", NB)
            for t in range(T):
                normalise(2 * NB - 2, 0, t)
            stage_b("end", NB, {})
            for t in range(T):
                normalise(2 * NB - 2, 1, t)

        @block.vector
        def _(dve):
            def row_max(kind, b, unit, parity, t, h):
                units.wait_full(dve, kind, b, unit)
                place = units.place(kind, unit)
                nc.vector.reduce_max(maxima[:, parity, h * T + t:h * T + t + 1], slots[place][:], AXIS_X)\
                  .then_inc(unit_free[place], 1)

            def split_max(kind, b, j, last_unit):
                units.wait_read(dve, kind, b, last_unit)
                n = b * (PAIRS * MAX_OPS) + (j + 1) * MAX_OPS
                m = maxima[:, (j + 1) % 2]
                part = [max_parts[:, i * 2 * T:(i + 1) * 2 * T] for i in range(PARTS)]
                nc.vector.tensor_scalar(part[0], m, -1.0, None, ALU.mult).then_inc(max_split, 1)
                dve.wait_ge(max_split, n + 1)
                nc.vector.scalar_tensor_tensor(max_rest[:], m, -1.0, part[0], ALU.mult, ALU.subtract)\
                  .then_inc(max_split, 1)
                dve.wait_ge(max_split, n + 2)
                nc.vector.tensor_copy(part[1], max_rest[:]).then_inc(max_split, 1)
                dve.wait_ge(max_split, n + 3)
                nc.vector.tensor_tensor(part[2], max_rest[:], part[1], ALU.subtract).then_inc(max_split, 1)

            def copy_max_rows(kind, b, j):
                unit = ("max rows", j)
                units.wait_full(dve, kind, b, unit)
                wait(dve, max_loaded, b * (PAIRS * 48) + (j + 1) * 48)
                nc.vector.tensor_copy(max_rows[:], t_bank[:].bitcast(BF16)[:, 0:P])\
                  .then_inc(unit_free[3], 1)

            def normalise_o(kind, b, j, pair):
                unit = ("O rows", j)
                units.wait_full(dve, kind, b, unit)
                o = t_bank[:].rearrange("p (g c) -> p g c", c=32)
                nc.vector.reciprocal(rden[:], o[:, :, D]).then_inc(reciprocal_done, 1)
                dve.wait_ge(reciprocal_done, b * PAIRS + (j + 1))
                if pair == 0:
                    wait(dve, sum_ready, b)
                nc.vector.tensor_tensor(attn[:, :, 2 * D * pair:2 * D * (pair + 1)]
                                        .rearrange("p t (h d) -> p t h d", d=D),
                                        o[:, :, 0:D].rearrange("p (t h) d -> p t h d", h=2),
                                        rden[:].rearrange("p (t h) -> p t h", h=2).unsqueeze(3)
                                        .to_broadcast([P, T, 2, D]), ALU.mult)\
                  .then_inc(unit_free[3], 1)

            def elu(kind, b, unit):
                units.wait_read(dve, kind, b, unit)
                c = 2 * (unit[1] % 2)
                nc.vector.scalar_tensor_tensor(work[:, c], work[:, c], 1.0, work[:, c + 1], ALU.min, ALU.add)\
                  .then_inc(elu_done, 1)

            def low_part(kind, b, unit, n):
                dve.wait_ge(hi_ready, b * HI_PER_BATCH + (n + 1 - HI_PER_BATCH))
                place = units.place(kind, unit)
                s = slots[place]
                if unit[0] == "hT":
                    c = unit[1]
                    ins = nc.vector.scalar_tensor_tensor(hT[:, 1, c, :], s[:], H_SCALE, hT[:, 0, c, :],
                                                         ALU.mult, ALU.subtract)
                else:
                    u = unit[2]
                    dst = h0T if unit[0] == "L0" else h1T
                    ins = nc.vector.scalar_tensor_tensor(dst[:, 1, 2 * u:2 * u + 2, :],
                                                         s[:].rearrange("p (i n) -> p i n", i=2), 0.0,
                                                         dst[:, 0, 2 * u:2 * u + 2, :], ALU.max, ALU.subtract)
                ins.then_inc(unit_free[place], 1)

            def v_out(kind, b, half):
                unit = ("V", half)
                units.wait_full(dve, kind, b, unit)
                if half == 0 and kind != "start":
                    dve.wait_ge(v_copied, b * PAIRS + PAIRS)
                    dve.wait_ge(lepe_done, b * LEPE_OPS + LEPE_OPS)
                place = units.place(kind, unit)
                nc.vector.tensor_tensor(v_ext[:, 1 + 4 * half:5 + 4 * half, :],
                                        slots[place][:].rearrange("p (t c) -> p t c", c=C),
                                        lepe_rows[:, 4].unsqueeze(1).to_broadcast([P, 4, C]), ALU.add)\
                  .then_inc(unit_free[place], 1)

            def ffn_residual(kind, b, th):
                unit = ("L2", th)
                units.wait_full(dve, kind, b, unit)
                place = units.place(kind, unit)
                h = hres[:, 4 * th:4 * th + 4, :]
                nc.vector.scalar_tensor_tensor(h, slots[place][:].rearrange("p (t c) -> p t c", c=C), out_scale, h,
                                               ALU.mult, ALU.add).then_inc(unit_free[place], 1)

            def stage_b(kind, b, after_unit):
                n = 0
                for i, unit in enumerate(b_units(kind not in ("start", "first"), kind not in ("last", "end"))):
                    if unit[0] == "V":
                        v_out(kind, b, unit[1])
                    elif unit[0] == "L2":
                        ffn_residual(kind, b, unit[1])
                    elif unit[0] == "proj":
                        elu(kind, b, unit)
                    else:
                        low_part(kind, b, unit, n)
                        n += 1
                    if i in after_unit:
                        after_unit[i]()

            def ln_tile(m2, which, t):
                nc.vector.bn_stats(stats[:, t, :], hres[:, t, :]).then_inc(ln_stats, 1)
                if t == T - 1:
                    for i in range(T):
                        if i == 0:
                            wait_apart(dve, ln_stats, (m2 + which) * LN_OPS + T, (dve_setup, 2))
                        nc.vector.bn_aggr(moments[:, i, :], stats[:, i, :]).then_inc(ln_stats, 1)

            nc.vector.memset(k_stack[STACK:P, :, :], 1.0)
            dve.wait_ge(pool_setup, 4)
            nc.vector.tensor_copy(ident16[:], ident[:]).then_inc(dve_setup, 1)
            nc.vector.memset(max_parts[:], 0.0).then_inc(dve_setup, 1)
            dve.wait_ge(k_loaded, 6 * 16)
            steps = [0]

            def then(ins):
                steps[0] += 1
                ins.then_inc(weights_ready, 1)
                dve.wait_ge(weights_ready, steps[0])

            then(nc.vector.tensor_scalar(s_sign[:], s_in[:], 0.0, 2.0, ALU.is_ge, ALU.mult))
            then(nc.vector.tensor_scalar(s_sign[:], s_sign[:], -1.0, None, ALU.add))
            then(nc.vector.tensor_scalar(s_work[:, 0:1], s_sign[:, 0:1], 2.0 * Y0_SCALE / H_SCALE, None, ALU.mult))
            then(nc.vector.tensor_scalar(s_work[:, 1:2], s_sign[:, 1:2], 2.0 * Y1_SCALE / Y0_SCALE, None, ALU.mult))
            then(nc.vector.tensor_scalar(s_work[:, 2:3], s_work[:, 1:2], -0.5, None, ALU.mult))
            then(nc.vector.tensor_tensor(s_work[:, 3:4], s_in[:, 0:1], s_sign[:, 0:1], ALU.mult))
            then(nc.vector.tensor_tensor(s_work[:, 4:5], s_in[:, 1:2], s_sign[:, 1:2], ALU.mult))
            then(nc.vector.tensor_tensor(s_work[:, 3:4], s_work[:, 3:4], s_work[:, 4:5], ALU.mult))
            then(nc.vector.scalar_tensor_tensor(out_scale, s_work[:, 3:4], 4.0 / Y1_SCALE, s_in[:, 2:3],
                                                ALU.mult, ALU.mult))
            then(nc.vector.tensor_tensor(w0[:], k0_u8[:, 0:KC], k0_u8[:, KC:2 * KC], ALU.subtract))
            then(nc.vector.tensor_scalar(w0[:], w0[:], s_work[:, 0:1], None, ALU.mult))
            then(nc.vector.tensor_scalar(w1[:], k1_u8, s_work[:, 1:2], s_work[:, 2:3], ALU.mult, ALU.add))
            then(nc.vector.tensor_scalar(w2[:], k2_u8, 2.0, -1.0, ALU.mult, ALU.add))

            dve.wait_ge(weights_loaded, 9 * 16)
            stage_b("start", 0, {})
            for v in range(T + LEAD):
                for h in range(2):
                    row_max("start", 0, ("S", -1, v, h), v // T, v % T, h)
                if v == T - 1:
                    split_max("start", 0, -1, ("S", -1, v, 1))
            copy_max_rows("start", 0, -1)

            def iteration(kind, b):
                for j in range(PAIRS):
                    if j == PAIRS // 2:
                        stage_b(kind, b, {1 if kind != "last" else 0: lambda: normalise_o(kind, b, j - 1, j - 1)})
                    for kt in range(T):
                        ahead = j * T + kt + T + LEAD
                        if kt == 5 and (kind != "last" or j < PAIRS - 1):
                            split_max(kind, b, j, ("S", j, 4, 1))
                        if kt == 6 and (kind != "last" or j < PAIRS - 1):
                            copy_max_rows(kind, b, j)
                        if has_scores(kind, j, kt):
                            for h in range(2):
                                row_max(kind, b, ("S", j, kt, h), (ahead // T) % 2, ahead % T, h)
                        if kt == 2 and j == 0 and kind != "first":
                            normalise_o(kind, b, -1, PAIRS - 1)
                        elif kt == 2 and j not in (0, PAIRS // 2):
                            normalise_o(kind, b, j - 1, j - 1)
                        if j == 1 and kind != "first":
                            if kt == 0:
                                dve.wait_ge(sum_ready, b)
                            ln_tile(b * 2 - 2, 0, kt)
                        if j == 4 and kind != "first":
                            if kt == 0:
                                units.wait_read(dve, kind, b, ("L2", 1))
                            ln_tile(b * 2 - 2, 1, kt)

            over_batches(dve, iteration)
            normalise_o("end", NB, -1, PAIRS - 1)
            dve.wait_ge(sum_ready, NB)
            for t in range(T):
                ln_tile(2 * NB - 2, 0, t)
            stage_b("end", NB, {})
            units.wait_read(dve, "end", NB, ("L2", 1))
            for t in range(T):
                ln_tile(2 * NB - 2, 1, t)

        @block.gpsimd
        def _(pool):
            combine = nc.gpsimd.tensor_tensor

            def rotate_and_split(kind, b, batch, which):
                g = (batch * 2 + which) * SPLIT_OPS
                pool.wait_ge(elu_done, batch * 4 + 2 * which + 2)
                A, B_, Cc, D_ = (work[:, i] for i in range(4))
                one = ln_consts[:, 0, 3:4].to_broadcast([P, N])
                n = [0]

                def step(ins, before_dma=False):
                    n[0] += 1
                    ins.then_inc(split_done, 1)
                    if before_dma:
                        wait_apart(pool, split_done, g + n[0], (pool_setup, 4))
                    else:
                        pool.wait_ge(split_done, g + n[0])

                step(combine(B_, Cc, sin_sb, ALU.mult))
                step(combine(D_, A, cos_sb, ALU.mult))
                step(combine(D_, D_, B_, ALU.subtract))
                step(combine(B_, A, sin_sb, ALU.mult))
                step(combine(Cc, Cc, cos_sb, ALU.mult))
                step(combine(B_, B_, Cc, ALU.add))
                scratch = (q_scratch, k_scratch)[which]
                for c, o in enumerate((D_, B_)):
                    sent = ((batch * 2 + which) * 2 + c) * 16
                    if not (isinstance(sent, int) and sent == 0):
                        pool.wait_ge(scratch_written, sent)
                    step(combine(parts[:, 0], o, one, ALU.mult))
                    step(combine(A, o, parts[:, 0], ALU.subtract))
                    step(combine(parts[:, 1], A, one, ALU.mult))
                    step(combine(parts[:, 2], A, parts[:, 1], ALU.subtract), before_dma=True)
                    pool.dma_start(scratch.ap()[batch, :, c].rearrange("t p n -> p t n"), parts[:])\
                        .then_inc(scratch_written, 16)

            def lepe(b):
                n = [0]
                tmp = work[:, 0:2].rearrange("p a (t c) -> p (a t) c", c=C)
                row = lambda i: lepe_rows[:, i].unsqueeze(1).to_broadcast([P, T, C])

                def step(ins):
                    n[0] += 1
                    ins.then_inc(lepe_done, 1)
                    pool.wait_ge(lepe_done, b * LEPE_OPS + n[0])

                pool.wait_ge(x_loaded, b * 16 + 16)
                pool.wait_ge(edges_loaded, b * 32 + 32)
                for k, tap in ((1, 1), (0, 0), (2, 2)):
                    step(combine(tmp, v_ext[:, k:k + T, :], row(tap), ALU.mult))
                    step(combine(base[:], base[:], tmp, ALU.add))
                step(combine(base[:], base[:], row(3), ALU.add))

            def add_attention(b_next):
                units.wait_read(pool, *b_next, ("O rows", -1))
                b = b_next[1]
                pool.wait_ge(out_stored, b * 16)
                combine(hres[:], attn[:], base[:], ALU.add).then_inc(sum_ready, 1)

            def ln_scales(m2, which):
                g = m2 + which
                pool.wait_ge(ln_stats, g * LN_OPS + LN_OPS)
                nc.gpsimd.tensor_tensor(neg_mean[:], moments[:, :, 0], ln_consts[:, :, 1], ALU.mult)
                nc.gpsimd.tensor_tensor(var_eps[:], moments[:, :, 1], ln_consts[:, :, 2], ALU.add)\
                    .then_inc(ln_scale, 1)
                pool.wait_ge(ln_scale, g * 3 + 1)
                nc.gpsimd.tensor_tensor(rstd[:], var_eps[:], ln_consts[:, :, 0], ALU.pow).then_inc(ln_scale, 1)
                pool.wait_ge(ln_scale, g * 3 + 2)
                nc.gpsimd.tensor_tensor(shift[:], neg_mean[:], rstd[:], ALU.mult).then_inc(ln_scale, 1)

            nc.gpsimd.memset(neg_mean[:], 0.0).then_inc(out_stored, 16)
            nc.gpsimd.memset(v_pair[:], 0.0).then_inc(pool_setup, 1)
            nc.gpsimd.memset(ident[:], 0.0).then_inc(pool_setup, 1)
            for i, c in enumerate((-0.5, -1.0, EPS, 1.0)):
                nc.gpsimd.memset(ln_consts[:, :, i], c)
            nc.gpsimd.memset(v_ext[:, 0, :], 0.0)
            nc.gpsimd.memset(v_ext[:, T + 1, :], 0.0)
            pool.wait_ge(pool_setup, 2)
            nc.gpsimd.memset(v_pair[:, :, :, :, D:D + 1], 1.0).then_inc(pool_setup, 1)
            nc.gpsimd.affine_select(out=ident[:], in_=ident[:], compare_op=ALU.not_equal, fill=1.0, base=0,
                                    pattern=[[-1, P]], channel_multiplier=1).then_inc(pool_setup, 1)
            pool.wait_ge(weights_loaded, 9 * 16)
            rotate_and_split("start", 0, 0, 0)
            rotate_and_split("start", 0, 0, 1)

            def iteration(kind, b):
                if kind != "first":
                    add_attention((kind, b))
                lepe(b)
                if kind != "first":
                    ln_scales(b * 2 - 2, 0)
                if kind != "last":
                    rotate_and_split(kind, b, b + 1, 0)
                    rotate_and_split(kind, b, b + 1, 1)
                if kind != "first":
                    ln_scales(b * 2 - 2, 1)

            over_batches(pool, iteration)
            add_attention(("end", NB))
            ln_scales(2 * NB - 2, 0)
            ln_scales(2 * NB - 2, 1)


def kernel(**inputs):
    import concourse.bacc as bacc
    from concourse.bass_utils import run_bass_kernel_spmd

    x = np.asarray(inputs["L0_attn_x"])
    w_qkv = np.asarray(inputs["L0_attn_w_qkv"])
    b_qkv = np.asarray(inputs["L0_attn_b_qkv"])
    order = np.concatenate([which * C + c + 2 * np.arange(D // 2)[:, None] + D * np.arange(H)[None, :]
                            for which in range(2) for c in range(2)]).reshape(-1)
    rows = np.concatenate([order, 2 * C + np.arange(C)])
    xT = x.reshape(NB, P, T, KC, P).transpose(0, 4, 3, 2, 1).reshape(NB, P, KC, N)
    position = (T * np.arange(P)[None, :] + np.arange(T)[:, None]).reshape(1, N).astype(np.float32)
    freq = np.exp(np.arange(0, D, 2, dtype=np.float32) * np.float32(-np.log(10000.0) / D)).astype(np.float32)
    angle = np.repeat(freq, H)[:, None] * position
    arrays = {
        "x": x.reshape(NB, P, T, C),
        "xT": np.concatenate([xT, xT[:1]]),
        "wT": w_qkv[rows].T.reshape(KC, P, 3 * C).transpose(1, 0, 2),
        "b_qk": b_qkv[order].reshape(4, P).T,
        "b_v": b_qkv[2 * C:],
        "w_lepe": np.asarray(inputs["L0_attn_w_lepe"]).reshape(C, 3).T,
        "b_lepe": np.asarray(inputs["L0_attn_b_lepe"]),
        "cos": np.cos(angle),
        "sin": np.sin(angle),
        "k0": np.asarray(inputs["L0_ffn_k0"]),
        "k1": np.asarray(inputs["L0_ffn_k1"]),
        "k2": np.asarray(inputs["L0_ffn_k2"]),
        "s0": np.asarray(inputs["L0_ffn_s0"]).reshape(1),
        "s1": np.asarray(inputs["L0_ffn_s1"]).reshape(1),
        "s2": np.asarray(inputs["L0_ffn_s2"]).reshape(1),
    }
    nc = bacc.Bacc("TRN2", target_bir_lowering=False, num_devices=1)
    aps, fed = {}, {}
    for name, a in arrays.items():
        a = np.ascontiguousarray(a)
        fed[f"in_{name}"] = a
        aps[name] = nc.dram_tensor(f"in_{name}", list(a.shape), mybir.dt.from_np(a.dtype), kind="ExternalInput").ap()
    aps["out"] = nc.dram_tensor("out_0", [NB, P, T, C], F32, kind="ExternalOutput").ap()
    build(nc, **aps)
    r = run_bass_kernel_spmd(nc, [fed], core_ids=[0])
    return np.asarray(r.results[0]["out_0"]).reshape(NB, N, C)
```

```python
from contextlib import ExitStack

import numpy as np
import concourse.bass as bass
from concourse import mybir

ALU = mybir.AluOpType
ACT = mybir.ActivationFunctionType
AXIS_XY = mybir.AxisListType.XY
F32 = mybir.dt.float32
BF16 = mybir.dt.bfloat16
F16 = mybir.dt.float16
U8 = mybir.dt.uint8

P = 128
NB, N, C = 8, 1024, 256
H, D = 16, 16
F = 1024
T = N // P
KC = C // P
KF = F // P
PAIRS = H // 2
RING = 4
LEAD = 3
PARTS = 3
STACK = 6 * D
Q_PART = (0, 0, 0, 1, 1, 2)
K_PART = (0, 1, 2, 0, 1, 0)
EPS = 1e-5
H_SCALE = 2.0 ** 11
Y0_SCALE = 2.0 ** 6
Y1_SCALE = 2.0 ** -4
HI_PER_BATCH = 2 + 4 * T // 2
SPLIT_OPS = 14
LEPE_OPS = 7
MAX_OPS = 4
LN_OPS = 2 * T
LOAD = 16 * 9

PROJ = ("qA", "qB", "kA", "kB")


def b_units(kind):
    ffn, proj = kind not in ("start", "first"), kind not in ("last", "end")
    l0 = lambda th: [("L0", th, u) for u in range(4)]
    l1 = lambda th: [("L1", th, u) for u in range(4)]
    order = [("hT", 0), ("hT", 1), ("proj", 0), ("proj", 1), *l0(0), *l1(0), ("proj", 2), ("proj", 3),
             *l0(1), ("L2", 0), *l1(1), ("V", 0), ("V", 1), ("L2", 1)]
    return [u for u in order if (proj if u[0] in ("proj", "V") else ffn)]


def has_scores(kind, j, kt):
    return kind != "last" or (j + 1) * T + kt + LEAD < PAIRS * T


def has_max_rows(kind, j):
    return kind != "last" or j < PAIRS - 1


def o_rows_pair(kind, j, kt):
    if kt == 2 and j != PAIRS // 2 and not (j == 0 and kind == "first"):
        return j - 1
    return None


def plan_units(kind):
    def attention(units, first):
        double, single = [(0, 1), (2, 3)], [(4,), (5,), (6,)]
        used = {2: 0, 1: 0}
        for u in units:
            n = 2 if u[0] == "S" else 1
            ring = double if n == 2 else single
            yield u, ring[used[n] % len(ring)]
            used[n] += 1

    def stage_b(extra=()):
        n = 0
        for i, u in enumerate(b_units(kind)):
            yield u, ((0, 1), (2, 3), (4, 5))[n % 3]
            n += 1
            if i == 1:
                yield from ((x, (6,)) for x in extra)

    if kind == "start":
        scores = [("S", -1, v, h) for v in range(T + LEAD) for h in range(2)]
        return [*stage_b(), *attention(scores + [("max rows", -1)], 0)]
    if kind == "end":
        return [(("O rows", -1), (6,)), *stage_b()]
    units = []
    for first in (0, PAIRS // 2):
        order = []
        for j in range(first, first + PAIRS // 2):
            for kt in range(T):
                for h in range(2):
                    if has_scores(kind, j, kt):
                        order.append(("S", j, kt, h))
                    order += [("T", j, kt, h, half) for half in range(2)]
                if o_rows_pair(kind, j, kt) is not None:
                    order.append(("O rows", j - 1))
                if kt == 5 and has_max_rows(kind, j):
                    order.append(("max rows", j))
        if first:
            units += stage_b([("O rows", first - 1)])
        units += attention(order, first)
    return units


READERS = {"S": ("dve", "dve"), "T": ("act", "act"), "proj": ("act", "act"), "hT": ("act", "dve"),
           "L0": ("act", "dve"), "L1": ("act", "dve"), "L2": ("dve", "dve"), "V": ("dve", "dve"),
           "O rows": ("dve", "dve"), "max rows": ("dve", "dve")}


class Units:

    BANKS = 7

    def __init__(self, psum, full, free):
        self.psum, self.full, self.free = psum, full, free
        self.bank, self.nth, self.before, self.total = {}, {}, {}, {}
        left = {}
        for kind, previous in (("start", None), ("first", "start"), ("mid", "first"), ("last", "mid"),
                               ("end", "last")):
            count = dict.fromkeys([("full", "act"), ("full", "dve"), ("free", "act"), ("free", "dve")], 0)
            user = dict(left.get(previous, {}))
            waited = {"act": -NB * N, "dve": -NB * N}
            for u, banks in plan_units(kind):
                first, last = READERS[u[0]]
                need = {}
                for e, n in (user[k] for k in banks if k in user):
                    if n > waited[e]:
                        need[e] = waited[e] = n
                count["full", first] += 1
                count["free", last] += 1
                self.bank[kind, u], self.before[kind, u] = banks, need
                self.nth[kind, u] = (count["full", first], count["free", last])
                for k in banks:
                    user[k] = (last, count["free", last])
            self.total[kind] = count
            left[kind] = {k: (e, n - count["free", e]) for k, (e, n) in user.items()}
        assert left["first"] == left["mid"]

    def count(self, kind, b, which, n):
        t = {k: v[which] for k, v in self.total.items()}
        if kind == "start":
            return n
        n += t["start"]
        if kind == "first":
            return n
        n += t["first"]
        if kind == "mid":
            return b * t["mid"] + (n - t["mid"])
        n += (NB - 2) * t["mid"]
        return n if kind == "last" else n + t["last"]

    def half(self, kind, unit, i):
        return self.psum[:, self.bank[kind, unit][i], :]

    def both(self, kind, unit):
        lo, hi = self.bank[kind, unit]
        return self.psum[:, lo:hi + 1, :]

    def full_sem(self, unit):
        return self.full[READERS[unit[0]][0]]

    def free_sem(self, unit):
        return self.free[READERS[unit[0]][1]]

    def wait_free(self, eng, kind, b, unit, source=None):
        need = dict(self.before[kind, unit])
        if source is not None:
            e = READERS[source[0]][1]
            need[e] = max(need.get(e, 0), self.nth[kind, source][1])
        for e, n in need.items():
            wait(eng, self.free[e], self.count(kind, b, ("free", e), n))

    def wait_full(self, eng, kind, b, unit):
        e = READERS[unit[0]][0]
        wait(eng, self.full[e], self.count(kind, b, ("full", e), self.nth[kind, unit][0]))

    def wait_read(self, eng, kind, b, unit):
        e = READERS[unit[0]][1]
        wait(eng, self.free[e], self.count(kind, b, ("free", e), self.nth[kind, unit][1]))

    def wait_previous_read(self, eng, kind, b, e):
        wait(eng, self.free[e], self.count(kind, b, ("free", e), 0))


def wait(eng, sem, value):
    if isinstance(value, int) and value <= 0:
        return
    eng.wait_ge(sem, value)


def wait_apart(eng, sem, value, long_over):
    if not isinstance(value, int):
        value = eng.to_reg(value)
    eng.wait_ge(*long_over)
    eng.wait_ge(sem, value)


def over_batches(eng, iteration):
    iteration("first", 0)
    with eng.Fori(1, NB - 1) as b:
        iteration("mid", b)
    iteration("last", NB - 1)


def build(nc, x, xT, wT, b_qk, b_v, w_lepe, b_lepe, cos, sin, k0, k1, k2, s0, s1, s2, out):
    with ExitStack() as ctx:
        def sb(name, shape, dt):
            return ctx.enter_context(nc.sbuf_tensor(name, shape, dt))

        def sem(name):
            return ctx.enter_context(nc.semaphore(name))

        q_scratch = nc.dram_tensor("q_scratch", [NB, PARTS, 2, P, N], BF16)
        k_scratch = nc.dram_tensor("k_scratch", [NB, PARTS, 2, P, N], BF16)

        q_stack = sb("q_stack", [P, RING, 2 * N], BF16)
        k_stack = sb("k_stack", [P, RING, 2 * N], BF16)
        v_pair = sb("v_pair", [P, RING, T, 2, 32], F32)
        v_ext = sb("v_ext", [P, T + 2, C], F32)
        xT_sb = sb("xT_sb", [P, KC, N], F32)
        base = sb("base", [P, T, C], F32)
        attn = sb("attn", [P, T, C], F32)
        hres = sb("hres", [P, T, C], F32)
        probs = sb("probs", [P, 4, N], F32)
        wT_sb = sb("wT_sb", [P, KC, 3 * C], F32)
        w0 = sb("w0", [P, KC, F], F16)
        w1 = sb("w1", [P, KF, F], F16)
        w2 = sb("w2", [P, KF, C], F16)
        rope = sb("rope", [P, 2, N], F32)
        cos_sb, sin_sb = rope[:, 0], rope[:, 1]
        work = sb("work", [P, 4, N], F32)
        parts = sb("parts", [P, PARTS, N], BF16)
        hT = sb("hT", [P, 2, KC, N], F16)
        h0T = sb("h0T", [P, 2, KF, N // 2], F16)
        h1T = sb("h1T", [P, 2, KF, N // 2], F16)
        o_sb = sb("o_sb", [P, 512], F32)
        lepe_rows = sb("lepe_rows", [P, 5, C], F32)
        ident = sb("ident", [P, P], F32)
        ident16 = sb("ident16", [P, P], BF16)
        bias_qk = sb("bias_qk", [P, 4], F32)
        maxima = sb("maxima", [P, 2, 2 * T], F32)
        max_rest = sb("max_rest", [P, 2 * T], F32)
        max_parts = sb("max_parts", [P, P], BF16)
        max_rows = sb("max_rows", [P, P], BF16)
        rden = sb("rden", [P, 2 * T], F32)
        stats = sb("stats", [P, T, 6], F32)
        moments = sb("moments", [P, T, 2], F32)
        var_eps = sb("var_eps", [P, T], F32)
        neg_mean = sb("neg_mean", [P, T], F32)
        ln_consts = sb("ln_consts", [P, T, 4], F32)
        rstd = sb("rstd", [P, T], F32)
        shift = sb("shift", [P, T], F32)
        s_in = sb("s_in", [P, 3], F32)
        s_sign = sb("s_sign", [P, 3], F32)
        s_work = sb("s_work", [P, 6], F32)
        out_scale = s_work[:, 5:6]
        stage0 = h0T[:].rearrange("p a k n -> p (a k n)").bitcast(U8)
        stage1 = h1T[:].rearrange("p a k n -> p (a k n)").bitcast(U8)
        k0_u8 = stage0[:, 0:2 * KC * F].rearrange("p (k n) -> p k n", n=F)
        k2_u8 = stage0[:, 2 * KC * F:2 * KC * F + KF * C].rearrange("p (k n) -> p k n", n=C)
        k1_u8 = stage1[:, 0:KF * F].rearrange("p (k n) -> p k n", n=F)

        unit_banks = ctx.enter_context(nc.psum_tensor("unit_banks", [P, Units.BANKS, 512], F32))
        o_bank = ctx.enter_context(nc.psum_tensor("o_bank", [P, 512], F32))

        unit_full = {e: sem(f"unit_full_for_{e}") for e in ("act", "dve")}
        unit_free = {e: sem(f"unit_read_by_{e}") for e in ("act", "dve")}
        weights_loaded = sem("weights_loaded")
        k_loaded = sem("k_loaded")
        xT_loaded = sem("xT_loaded")
        x_loaded = sem("x_loaded")
        stack_loaded = [sem(f"stack_loaded{i}") for i in range(RING)]
        max_loaded = sem("max_loaded")
        edges_loaded = sem("edges_loaded")
        scratch_written = sem("scratch_written")
        out_stored = sem("out_stored")
        pool_setup = sem("pool_setup")
        dve_setup = sem("dve_setup")
        weights_ready = sem("weights_ready")
        max_split = sem("max_split")
        pv_done = sem("pv_done")
        o_copied = sem("o_copied")
        v_copied = sem("v_copied")
        reciprocal_done = sem("reciprocal_done")
        attn_written = sem("attn_written")
        sum_ready = sem("sum_ready")
        lepe_done = sem("lepe_done")
        elu_done = sem("elu_done")
        split_done = sem("split_done")
        ln_stats = sem("ln_stats")
        ln_scale = sem("ln_scale")
        ln_done = sem("ln_done")
        hi_ready = sem("hi_ready")
        units = Units(unit_banks, unit_full, unit_free)

        block = ctx.enter_context(nc.Block())

        q_rows = q_scratch.ap().rearrange("b t c (i h) n -> b (t c i) (h n)", h=H)
        k_rows = k_scratch.ap().rearrange("b t c (i h) n -> b (t c i) (h n)", h=H)

        @block.sync
        def _(sp):
            def load_stacks(b, j):
                r = j % RING
                cols = slice(j * 2 * N, (j + 1) * 2 * N)
                for blk, part in enumerate(Q_PART):
                    sp.dma_start(q_stack[blk * D:(blk + 1) * D, r], q_rows[b, part * D:(part + 1) * D, cols])\
                      .then_inc(stack_loaded[r], 16)
                for blk, n in ((0, 3), (3, 2), (5, 1)):
                    sp.dma_start(k_stack[blk * D:(blk + n) * D, r], k_rows[b, 0:n * D, cols])\
                      .then_inc(stack_loaded[r], 16)

            def load_max(kind, b, j):
                units.wait_read(sp, kind, b, ("max rows", j))
                for p in range(PARTS):
                    sp.dma_start(q_stack[STACK + p:STACK + p + 1, (j + 1) % RING].rearrange("o (r q) -> o r q", q=P),
                                 max_rows[p * 2 * T:(p + 1) * 2 * T, :]).then_inc(max_loaded, 16)

            def load_edges(kind, b):
                units.wait_read(sp, kind, b, ("V", 1))
                sp.dma_start(v_ext[1:P, 0, :], v_ext[0:P - 1, T, :]).then_inc(edges_loaded, 16)
                sp.dma_start(v_ext[0:P - 1, T + 1, :], v_ext[1:P, 1, :]).then_inc(edges_loaded, 16)

            def store_out(m):
                sp.wait_ge(ln_done, (m * 2 + 2) * T)
                sp.dma_start(out[m], hres[:]).then_inc(out_stored, 16)

            sp.dma_start(xT_sb[:], xT[0]).then_inc(xT_loaded, 16)
            sp.dma_start(wT_sb[:], wT).then_inc(weights_loaded, 16)
            sp.dma_start(bias_qk[:], b_qk).then_inc(weights_loaded, 16)
            sp.dma_start(rope[:, 0], cos).then_inc(weights_loaded, 16)
            sp.dma_start(rope[:, 1], sin).then_inc(weights_loaded, 16)
            for i in range(3):
                sp.dma_start(lepe_rows[:, i], w_lepe[i].partition_broadcast(P)).then_inc(weights_loaded, 16)
            sp.dma_start(lepe_rows[:, 3], b_lepe.partition_broadcast(P)).then_inc(weights_loaded, 16)
            sp.dma_start(lepe_rows[:, 4], b_v.partition_broadcast(P)).then_inc(weights_loaded, 16)
            for i, s in enumerate((s0, s1, s2)):
                sp.dma_start(s_in[:, i:i + 1], s.partition_broadcast(P)).then_inc(k_loaded, 16)
            sp.dma_start(k0_u8, k0.rearrange("(k p) n -> p k n", p=P)).then_inc(k_loaded, 16)
            sp.dma_start(k1_u8, k1.rearrange("(k p) n -> p k n", p=P)).then_inc(k_loaded, 16)
            sp.dma_start(k2_u8, k2.rearrange("(k p) n -> p k n", p=P)).then_inc(k_loaded, 16)
            units.wait_full(sp, "start", 0, ("V", 1))
            sp.dma_start(xT_sb[:], xT[1]).then_inc(xT_loaded, 16)
            load_edges("start", 0)
            sp.wait_ge(scratch_written, 4 * 16)
            for j in range(RING):
                load_stacks(0, j)
            load_max("start", 0, -1)

            def iteration(kind, b):
                for j in range(PAIRS):
                    if j == PAIRS // 2 and kind != "last":
                        load_edges(kind, b)
                        if kind == "first":
                            units.wait_full(sp, kind, b, ("V", 1))
                            sp.dma_start(xT_sb[:], xT[2]).then_inc(xT_loaded, 16)
                        else:
                            units.wait_full(sp, kind, b, ("V", 1))
                            sp.dma_start(xT_sb[:], xT[b + 2]).then_inc(xT_loaded, 16)
                    if kind != "last" or j < PAIRS - 1:
                        load_max(kind, b, j)
                    if j == 6 and kind != "first":
                        store_out(b - 1)
                    if kind == "last" and j + RING >= PAIRS:
                        continue
                    units.wait_full(sp, kind, b, ("T", j, T - 1, 1, 1))
                    if j + RING < PAIRS:
                        load_stacks(b, j + RING)
                    else:
                        sp.wait_ge(scratch_written, b * 64 + 128)
                        load_stacks(b + 1, j + RING - PAIRS)

            over_batches(sp, iteration)
            store_out(NB - 1)
            sp.wait_ge(out_stored, 16 * (NB + 1))

        @block.tensor
        def _(pe):
            def scores(kind, b, unit, j, t, h):
                r = j % RING
                units.wait_free(pe, kind, b, unit)
                for half in range(2):
                    last = nc.tensor.matmul(units.half(kind, unit, half),
                                            q_stack[0:STACK, r, h * N + t * P:h * N + (t + 1) * P],
                                            k_stack[0:STACK, r, h * N + half * 512:h * N + (half + 1) * 512],
                                            start=True, stop=True)
                last.then_inc(units.full_sem(unit), 1)

            def scores_T(kind, b, j, kt, h):
                r, rows = j % RING, STACK + PARTS
                for half in range(2):
                    unit = ("T", j, kt, h, half)
                    units.wait_free(pe, kind, b, unit)
                    nc.tensor.matmul(units.half(kind, unit, 0),
                                     k_stack[0:rows, r, h * N + kt * P:h * N + (kt + 1) * P],
                                     q_stack[0:rows, r, h * N + half * 512:h * N + (half + 1) * 512],
                                     start=True, stop=True).then_inc(units.full_sem(unit), 1)

            def weighted_v(kind, b, j, kt, part):
                if part == 0:
                    if j < 0:
                        units.wait_previous_read(pe, kind, b, "act")
                    else:
                        units.wait_read(pe, kind, b, ("T", j, kt, 1, 1))
                    if kt == 0:
                        wait(pe, v_copied, b * PAIRS + (j + 1))
                        wait(pe, o_copied, b * PAIRS + j)
                for parity in range(2):
                    for h in range(2):
                        g = 2 * parity + h
                        p = probs[:, 2 * (kt % 2) + h].rearrange("p (b f q) -> p b f q", f=2, q=P)
                        o = o_bank[32 * g:32 * g + 32, :].rearrange("p (b q) -> p b q", q=P)
                        last = nc.tensor.matmul(o[:, 2 * part:2 * part + 2, :], v_pair[:, j % RING, kt, h, :],
                                                p[:, 2 * part:2 * part + 2, parity, :],
                                                start=kt == 0 and part == 0, stop=kt == T - 1 and part == 1,
                                                skip_group_check=True)
                if part == 1:
                    last.then_inc(pv_done, 1)

            def max_rows_T(kind, b, j):
                unit = ("max rows", j)
                wait(pe, max_split, b * (PAIRS * MAX_OPS) + (j + 2) * MAX_OPS)
                units.wait_free(pe, kind, b, unit)
                nc.tensor.transpose(units.half(kind, unit, 0).bitcast(BF16)[:, 0:P], max_parts[:], ident16[:])\
                  .then_inc(units.full_sem(unit), 1)

            def o_rows(kind, b, j):
                unit = ("O rows", j)
                pe.wait_ge(o_copied, b * PAIRS + (j + 1))
                units.wait_free(pe, kind, b, unit)
                for blk in range(4):
                    last = nc.tensor.transpose(units.half(kind, unit, 0)[:, blk * P:(blk + 1) * P],
                                               o_sb[:, blk * P:(blk + 1) * P], ident[:])
                last.then_inc(units.full_sem(unit), 1)

            def project(kind, b, ct):
                unit = ("proj", ct)
                units.wait_free(pe, kind, b, unit)
                for half in range(2):
                    for kc in range(KC):
                        last = nc.tensor.matmul(units.half(kind, unit, half),
                                                wT_sb[:, kc, ct * P:(ct + 1) * P],
                                                xT_sb[:, kc, half * 512:(half + 1) * 512],
                                                start=kc == 0, stop=kc == KC - 1)
                last.then_inc(units.full_sem(unit), 1)

            def project_v(kind, b, half):
                unit = ("V", half)
                units.wait_free(pe, kind, b, unit)
                for t in range(4):
                    for kc in range(KC):
                        col = (4 * half + t) * P
                        last = nc.tensor.matmul(units.half(kind, unit, t // 2)[:, t % 2 * C:(t % 2 + 1) * C], xT_sb[:, kc, col:col + P],
                                                wT_sb[:, kc, 2 * C:3 * C], start=kc == 0, stop=kc == KC - 1)
                last.then_inc(units.full_sem(unit), 1)

            def transpose_h(kind, b, kc):
                unit = ("hT", kc)
                units.wait_free(pe, kind, b, unit)
                for t in range(T):
                    last = nc.tensor.transpose(units.half(kind, unit, t // 4)[:, t % 4 * P:(t % 4 + 1) * P], hres[:, t, kc * P:(kc + 1) * P], ident[:])
                last.then_inc(units.full_sem(unit), 1)

            def hidden(kind, b, layer, th, u):
                unit = (layer, th, u)
                tiles = KC if layer == "L0" else KF
                for k in range(tiles):
                    source = ("hT", 1) if layer == "L0" else ("L0", th, k // 2)
                    if k == 0:
                        units.wait_free(pe, kind, b, unit, source)
                    elif layer == "L1" and k % 2 == 0:
                        units.wait_read(pe, kind, b, source)
                    for i in range(2):
                        m = (2 * u + i) * P
                        for part in range(2):
                            if layer == "L0":
                                w, a = w0[:, k, m:m + P], hT[:, part, k, th * 512:(th + 1) * 512]
                            else:
                                w, a = w1[:, k, m:m + P], h0T[:, part, k, :]
                            last = nc.tensor.matmul(units.half(kind, unit, i), w, a,
                                                    start=k == 0 and part == 0,
                                                    stop=k == tiles - 1 and part == 1)
                last.then_inc(units.full_sem(unit), 1)

            def ffn_out(kind, b, th):
                unit = ("L2", th)
                units.wait_free(pe, kind, b, unit, ("L1", th, 3))
                for t in range(4):
                    for k in range(KF):
                        for part in range(2):
                            last = nc.tensor.matmul(units.half(kind, unit, t // 2)[:, t % 2 * C:(t % 2 + 1) * C],
                                                    h1T[:, part, k, t * P:(t + 1) * P],
                                                    w2[:, k, :], start=k == 0 and part == 0,
                                                    stop=k == KF - 1 and part == 1)
                last.then_inc(units.full_sem(unit), 1)

            def stage_b(kind, b, after_unit):
                for n, unit in enumerate(b_units(kind)):
                    if unit == ("hT", 0):
                        pe.wait_ge(ln_done, b * (2 * T) - T)
                    if unit == ("proj", 0):
                        pe.wait_ge(xT_loaded, b * 16 + 32 if kind != "start" else 16)
                    if unit[0] == "proj":
                        project(kind, b, unit[1])
                    elif unit[0] == "V":
                        project_v(kind, b, unit[1])
                    elif unit[0] == "hT":
                        transpose_h(kind, b, unit[1])
                    elif unit[0] == "L2":
                        ffn_out(kind, b, unit[1])
                    else:
                        hidden(kind, b, *unit)
                    if n in after_unit:
                        after_unit[n]()

            def stack_uses(b, j):
                return (b * (PAIRS // RING) + (j // RING + 1)) * LOAD

            pe.wait_ge(weights_loaded, 9 * 16)
            pe.wait_ge(pool_setup, 4)
            stage_b("start", 0, {})
            for v in range(T + LEAD):
                j = v // T
                if v % T == 0:
                    pe.wait_ge(stack_loaded[j], stack_uses(0, j))
                if v == 0:
                    pe.wait_ge(dve_setup, 2)
                for h in range(2):
                    scores("start", 0, ("S", -1, v, h), j, v % T, h)
            max_rows_T("start", 0, -1)

            def iteration(kind, b):
                for j in range(PAIRS):
                    if j == PAIRS // 2:
                        stage_b(kind, b, {0: lambda: [weighted_v(kind, b, j - 1, T - 1, part) for part in range(2)],
                                          1: lambda: o_rows(kind, b, j - 1)})
                    for kt in range(T):
                        ahead = j * T + kt + T + LEAD
                        if kt == 0:
                            pe.wait_ge(max_loaded, b * (PAIRS * 48) + (j + 1) * 48)
                        if ahead % T == 0 and has_scores(kind, j, kt):
                            n = ahead // T
                            pe.wait_ge(stack_loaded[n % RING], stack_uses(b, n))
                        for h in range(2):
                            if has_scores(kind, j, kt):
                                scores(kind, b, ("S", j, kt, h), ahead // T, ahead % T, h)
                            scores_T(kind, b, j, kt, h)
                            if kt > 0:
                                weighted_v(kind, b, j, kt - 1, h)
                            elif j != PAIRS // 2 and not (j == 0 and kind == "first"):
                                weighted_v(kind, b, j - 1, T - 1, h)
                        if o_rows_pair(kind, j, kt) is not None:
                            o_rows(kind, b, j - 1)
                        if kt == 5 and has_max_rows(kind, j):
                            max_rows_T(kind, b, j)

            over_batches(pe, iteration)
            for part in range(2):
                weighted_v("end", NB, -1, T - 1, part)
            o_rows("end", NB, -1)
            stage_b("end", NB, {})

        @block.scalar
        def _(act):
            def exp_probs(kind, b, j, kt, h):
                for half in range(2):
                    unit = ("T", j, kt, h, half)
                    units.wait_full(act, kind, b, unit)
                    if h == 0 and half == 0:
                        wait(act, pv_done, b * (PAIRS * T) + (j * T + kt - 1))
                    nc.scalar.activation(probs[:, 2 * (kt % 2) + h, half * 512:(half + 1) * 512],
                                         units.half(kind, unit, 0), ACT.Exp, scale=float(D) ** -0.5)\
                      .then_inc(units.free_sem(unit), 1)

            def copy_o(kind, b, j):
                act.wait_ge(pv_done, b * (PAIRS * T) + (j + 1) * T)
                before = b * PAIRS + j
                if not (isinstance(before, int) and before == 0):
                    wait_o_rows(kind, b, j)
                nc.scalar.activation(o_sb[:], o_bank[:], ACT.Copy).then_inc(o_copied, 1)

            def wait_o_rows(kind, b, j):
                act.wait_ge(reciprocal_done, b * PAIRS + j)

            def copy_v(b, j):
                if not (isinstance(b, int) and b == 0 and j < RING):
                    act.wait_ge(pv_done, b * (PAIRS * T) + (j - RING + 1) * T)
                nc.scalar.activation(v_pair[:, j % RING, :, :, 0:D],
                                     v_ext[:, 1:T + 1, 2 * D * j:2 * D * (j + 1)]
                                     .rearrange("p t (h d) -> p t h d", d=D), ACT.Copy).then_inc(v_copied, 1)

            def tail(kind, b, j):
                copy_o(kind, b, j)
                n = j + RING
                if n < PAIRS:
                    copy_v(b, n)
                elif kind != "last":
                    if j == RING:
                        units.wait_read(act, kind, b, ("V", 1))
                    copy_v(b + 1, n - PAIRS)

            def elu_inputs(kind, b, ct):
                unit = ("proj", ct)
                units.wait_full(act, kind, b, unit)
                if ct % 2 == 0:
                    if kind != "start":
                        act.wait_ge(lepe_done, b * LEPE_OPS + LEPE_OPS)
                        act.wait_ge(split_done, b * (2 * SPLIT_OPS) + (2 + ct // 2) * SPLIT_OPS)
                    elif ct:
                        act.wait_ge(split_done, SPLIT_OPS)
                for i, f in ((0, ACT.Exp), (1, ACT.Relu)):
                    last = nc.scalar.activation(work[:, 2 * (ct % 2) + i].rearrange("p (a n) -> p a n", a=2),
                                                units.both(kind, unit), f, bias=bias_qk[:, ct:ct + 1])
                last.then_inc(units.free_sem(unit), 1)

            def high_part(kind, b, unit):
                units.wait_full(act, kind, b, unit)
                s = units.both(kind, unit)
                if unit[0] == "hT":
                    ins = nc.scalar.activation(hT[:, 0, unit[1], :].rearrange("p (a n) -> p a n", a=2), s,
                                               ACT.Copy, scale=H_SCALE)
                else:
                    u = unit[2]
                    dst = h0T if unit[0] == "L0" else h1T
                    ins = nc.scalar.activation(dst[:, 0, 2 * u:2 * u + 2, :], s, ACT.Relu)
                ins.then_inc(hi_ready, 1)

            def stage_b(kind, b, after_unit):
                for n, unit in enumerate(b_units(kind)):
                    if unit[0] == "proj":
                        elu_inputs(kind, b, unit[1])
                    elif unit[0] in ("hT", "L0", "L1"):
                        high_part(kind, b, unit)
                    if n in after_unit:
                        after_unit[n]()

            def normalise(m2, which, t):
                if t == 0:
                    act.wait_ge(ln_scale, (m2 + which + 1) * 3)
                nc.scalar.activation(hres[:, t, :], hres[:, t, :], ACT.Identity, bias=shift[:, t:t + 1],
                                     scale=rstd[:, t:t + 1]).then_inc(ln_done, 1)

            act.wait_ge(weights_loaded, 9 * 16)
            stage_b("start", 0, {})
            act.wait_ge(pool_setup, 4)
            units.wait_read(act, "start", 0, ("V", 1))
            for j in range(RING):
                copy_v(0, j)

            def iteration(kind, b):
                for j in range(PAIRS):
                    if j == PAIRS // 2:
                        stage_b(kind, b, {0: lambda: tail(kind, b, j - 1)})
                    for kt in range(T):
                        for h in range(2):
                            exp_probs(kind, b, j, kt, h)
                        if kt == 0 and j == 0 and kind != "first":
                            tail_of_previous(kind, b)
                        elif kt == 0 and j not in (0, PAIRS // 2):
                            tail(kind, b, j - 1)
                        if j == 2 and kind != "first":
                            normalise(b * 2 - 2, 0, kt)
                        if j == 5 and kind != "first":
                            normalise(b * 2 - 2, 1, kt)

            def tail_of_previous(kind, b):
                copy_o(kind, b, -1)
                if kind != "end":
                    copy_v(b, RING - 1)

            over_batches(act, iteration)
            tail_of_previous("end", NB)
            for t in range(T):
                normalise(2 * NB - 2, 0, t)
            stage_b("end", NB, {})
            for t in range(T):
                normalise(2 * NB - 2, 1, t)

        @block.vector
        def _(dve):
            def row_max(kind, b, unit, parity, t, h):
                units.wait_full(dve, kind, b, unit)
                nc.vector.reduce_max(maxima[:, parity, h * T + t:h * T + t + 1], units.both(kind, unit), AXIS_XY)\
                  .then_inc(units.free_sem(unit), 1)

            def split_max(kind, b, j, last_unit):
                units.wait_read(dve, kind, b, last_unit)
                n = b * (PAIRS * MAX_OPS) + (j + 1) * MAX_OPS
                m = maxima[:, (j + 1) % 2]
                part = [max_parts[:, i * 2 * T:(i + 1) * 2 * T] for i in range(PARTS)]
                nc.vector.tensor_scalar(part[0], m, -1.0, None, ALU.mult).then_inc(max_split, 1)
                dve.wait_ge(max_split, n + 1)
                nc.vector.scalar_tensor_tensor(max_rest[:], m, -1.0, part[0], ALU.mult, ALU.subtract)\
                  .then_inc(max_split, 1)
                dve.wait_ge(max_split, n + 2)
                nc.vector.tensor_copy(part[1], max_rest[:]).then_inc(max_split, 1)
                dve.wait_ge(max_split, n + 3)
                nc.vector.tensor_tensor(part[2], max_rest[:], part[1], ALU.subtract).then_inc(max_split, 1)

            def copy_max_rows(kind, b, j):
                unit = ("max rows", j)
                units.wait_full(dve, kind, b, unit)
                wait(dve, max_loaded, b * (PAIRS * 48) + (j + 1) * 48)
                nc.vector.tensor_copy(max_rows[:], units.half(kind, unit, 0).bitcast(BF16)[:, 0:P])\
                  .then_inc(units.free_sem(unit), 1)

            def normalise_o(kind, b, j, pair):
                unit = ("O rows", j)
                units.wait_full(dve, kind, b, unit)
                o = units.half(kind, unit, 0).rearrange("p (g c) -> p g c", c=32)
                nc.vector.reciprocal(rden[:], o[:, :, D]).then_inc(reciprocal_done, 1)
                dve.wait_ge(reciprocal_done, b * PAIRS + (j + 1))
                if pair == 0:
                    wait(dve, sum_ready, b)
                nc.vector.tensor_tensor(attn[:, :, 2 * D * pair:2 * D * (pair + 1)]
                                        .rearrange("p t (h d) -> p t h d", d=D),
                                        o[:, :, 0:D].rearrange("p (t h) d -> p t h d", h=2),
                                        rden[:].rearrange("p (t h) -> p t h", h=2).unsqueeze(3)
                                        .to_broadcast([P, T, 2, D]), ALU.mult)\
                  .then_inc(units.free_sem(unit), 1)

            def elu(kind, b, unit):
                units.wait_read(dve, kind, b, unit)
                c = 2 * (unit[1] % 2)
                nc.vector.scalar_tensor_tensor(work[:, c], work[:, c], 1.0, work[:, c + 1], ALU.min, ALU.add)\
                  .then_inc(elu_done, 1)

            def low_part(kind, b, unit, n):
                dve.wait_ge(hi_ready, b * HI_PER_BATCH + (n + 1 - HI_PER_BATCH))
                s = units.both(kind, unit)
                if unit[0] == "hT":
                    hi, lo = (hT[:, i, unit[1], :].rearrange("p (a n) -> p a n", a=2) for i in range(2))
                    ins = nc.vector.scalar_tensor_tensor(lo, s, H_SCALE, hi, ALU.mult, ALU.subtract)
                else:
                    u = unit[2]
                    dst = h0T if unit[0] == "L0" else h1T
                    ins = nc.vector.scalar_tensor_tensor(dst[:, 1, 2 * u:2 * u + 2, :],
                                                         s, 0.0, dst[:, 0, 2 * u:2 * u + 2, :], ALU.max, ALU.subtract)
                ins.then_inc(units.free_sem(unit), 1)

            def v_out(kind, b, half):
                unit = ("V", half)
                units.wait_full(dve, kind, b, unit)
                if half == 0 and kind != "start":
                    dve.wait_ge(v_copied, b * PAIRS + PAIRS)
                    dve.wait_ge(lepe_done, b * LEPE_OPS + LEPE_OPS)
                nc.vector.tensor_tensor(v_ext[:, 1 + 4 * half:5 + 4 * half, :].rearrange("p (a t) c -> p a t c", a=2),
                                        units.both(kind, unit).rearrange("p a (t c) -> p a t c", c=C),
                                        lepe_rows[:, 4:5].unsqueeze(1).to_broadcast([P, 2, 2, C]), ALU.add)\
                  .then_inc(units.free_sem(unit), 1)

            def ffn_residual(kind, b, th):
                unit = ("L2", th)
                units.wait_full(dve, kind, b, unit)
                h = hres[:, 4 * th:4 * th + 4, :].rearrange("p (a t) c -> p a t c", a=2)
                nc.vector.scalar_tensor_tensor(h, units.both(kind, unit).rearrange("p a (t c) -> p a t c", c=C),
                                               out_scale, h, ALU.mult, ALU.add).then_inc(units.free_sem(unit), 1)

            def stage_b(kind, b, after_unit):
                n = 0
                for i, unit in enumerate(b_units(kind)):
                    if unit[0] == "V":
                        v_out(kind, b, unit[1])
                    elif unit[0] == "L2":
                        ffn_residual(kind, b, unit[1])
                    elif unit[0] == "proj":
                        elu(kind, b, unit)
                    else:
                        low_part(kind, b, unit, n)
                        n += 1
                    if i in after_unit:
                        after_unit[i]()

            def ln_tile(m2, which, t):
                nc.vector.bn_stats(stats[:, t, :], hres[:, t, :]).then_inc(ln_stats, 1)
                if t == T - 1:
                    for i in range(T):
                        if i == 0:
                            wait_apart(dve, ln_stats, (m2 + which) * LN_OPS + T, (dve_setup, 2))
                        nc.vector.bn_aggr(moments[:, i, :], stats[:, i, :]).then_inc(ln_stats, 1)

            nc.vector.memset(k_stack[STACK:P, :, :], 1.0)
            dve.wait_ge(pool_setup, 4)
            nc.vector.tensor_copy(ident16[:], ident[:]).then_inc(dve_setup, 1)
            nc.vector.memset(max_parts[:], 0.0).then_inc(dve_setup, 1)
            dve.wait_ge(k_loaded, 6 * 16)
            steps = [0]

            def then(ins):
                steps[0] += 1
                ins.then_inc(weights_ready, 1)
                dve.wait_ge(weights_ready, steps[0])

            then(nc.vector.tensor_scalar(s_sign[:], s_in[:], 0.0, 2.0, ALU.is_ge, ALU.mult))
            then(nc.vector.tensor_scalar(s_sign[:], s_sign[:], -1.0, None, ALU.add))
            then(nc.vector.tensor_scalar(s_work[:, 0:1], s_sign[:, 0:1], 2.0 * Y0_SCALE / H_SCALE, None, ALU.mult))
            then(nc.vector.tensor_scalar(s_work[:, 1:2], s_sign[:, 1:2], 2.0 * Y1_SCALE / Y0_SCALE, None, ALU.mult))
            then(nc.vector.tensor_scalar(s_work[:, 2:3], s_work[:, 1:2], -0.5, None, ALU.mult))
            then(nc.vector.tensor_tensor(s_work[:, 3:4], s_in[:, 0:1], s_sign[:, 0:1], ALU.mult))
            then(nc.vector.tensor_tensor(s_work[:, 4:5], s_in[:, 1:2], s_sign[:, 1:2], ALU.mult))
            then(nc.vector.tensor_tensor(s_work[:, 3:4], s_work[:, 3:4], s_work[:, 4:5], ALU.mult))
            then(nc.vector.scalar_tensor_tensor(out_scale, s_work[:, 3:4], 4.0 / Y1_SCALE, s_in[:, 2:3],
                                                ALU.mult, ALU.mult))
            then(nc.vector.tensor_tensor(w0[:], k0_u8[:, 0:KC], k0_u8[:, KC:2 * KC], ALU.subtract))
            then(nc.vector.tensor_scalar(w0[:], w0[:], s_work[:, 0:1], None, ALU.mult))
            then(nc.vector.tensor_scalar(w1[:], k1_u8, s_work[:, 1:2], s_work[:, 2:3], ALU.mult, ALU.add))
            then(nc.vector.tensor_scalar(w2[:], k2_u8, 2.0, -1.0, ALU.mult, ALU.add))

            dve.wait_ge(weights_loaded, 9 * 16)
            stage_b("start", 0, {})
            for v in range(T + LEAD):
                for h in range(2):
                    row_max("start", 0, ("S", -1, v, h), v // T, v % T, h)
                if v == T - 1:
                    split_max("start", 0, -1, ("S", -1, v, 1))
            copy_max_rows("start", 0, -1)

            def iteration(kind, b):
                for j in range(PAIRS):
                    if j == PAIRS // 2:
                        stage_b(kind, b, {1: lambda: normalise_o(kind, b, j - 1, j - 1)})
                    for kt in range(T):
                        ahead = j * T + kt + T + LEAD
                        if kt == 5 and has_max_rows(kind, j):
                            split_max(kind, b, j, ("S", j, 4, 1))
                        if kt == 6 and has_max_rows(kind, j):
                            copy_max_rows(kind, b, j)
                        if has_scores(kind, j, kt):
                            for h in range(2):
                                row_max(kind, b, ("S", j, kt, h), (ahead // T) % 2, ahead % T, h)
                        if kt == 2 and j == 0 and kind != "first":
                            normalise_o(kind, b, -1, PAIRS - 1)
                        elif kt == 2 and j not in (0, PAIRS // 2):
                            normalise_o(kind, b, j - 1, j - 1)
                        if j == 1 and kind != "first":
                            if kt == 0:
                                dve.wait_ge(sum_ready, b)
                            ln_tile(b * 2 - 2, 0, kt)
                        if j == 4 and kind != "first":
                            if kt == 0:
                                units.wait_read(dve, kind, b, ("L2", 1))
                            ln_tile(b * 2 - 2, 1, kt)

            over_batches(dve, iteration)
            normalise_o("end", NB, -1, PAIRS - 1)
            dve.wait_ge(sum_ready, NB)
            for t in range(T):
                ln_tile(2 * NB - 2, 0, t)
            stage_b("end", NB, {})
            units.wait_read(dve, "end", NB, ("L2", 1))
            for t in range(T):
                ln_tile(2 * NB - 2, 1, t)

        @block.gpsimd
        def _(pool):
            combine = nc.gpsimd.tensor_tensor

            def rotate_and_split(kind, b, batch, which):
                g = (batch * 2 + which) * SPLIT_OPS
                pool.wait_ge(elu_done, batch * 4 + 2 * which + 2)
                A, B_, Cc, D_ = (work[:, i] for i in range(4))
                one = ln_consts[:, 0, 3:4].to_broadcast([P, N])
                n = [0]

                def step(ins, before_dma=False):
                    n[0] += 1
                    ins.then_inc(split_done, 1)
                    if before_dma:
                        wait_apart(pool, split_done, g + n[0], (pool_setup, 4))
                    else:
                        pool.wait_ge(split_done, g + n[0])

                step(combine(B_, Cc, sin_sb, ALU.mult))
                step(combine(D_, A, cos_sb, ALU.mult))
                step(combine(D_, D_, B_, ALU.subtract))
                step(combine(B_, A, sin_sb, ALU.mult))
                step(combine(Cc, Cc, cos_sb, ALU.mult))
                step(combine(B_, B_, Cc, ALU.add))
                scratch = (q_scratch, k_scratch)[which]
                for c, o in enumerate((D_, B_)):
                    sent = ((batch * 2 + which) * 2 + c) * 16
                    if not (isinstance(sent, int) and sent == 0):
                        pool.wait_ge(scratch_written, sent)
                    step(combine(parts[:, 0], o, one, ALU.mult))
                    step(combine(A, o, parts[:, 0], ALU.subtract))
                    step(combine(parts[:, 1], A, one, ALU.mult))
                    step(combine(parts[:, 2], A, parts[:, 1], ALU.subtract), before_dma=True)
                    pool.dma_start(scratch.ap()[batch, :, c].rearrange("t p n -> p t n"), parts[:])\
                        .then_inc(scratch_written, 16)

            def lepe(b):
                n = [0]
                tmp = work[:, 0:2].rearrange("p a (t c) -> p (a t) c", c=C)
                row = lambda i: lepe_rows[:, i].unsqueeze(1).to_broadcast([P, T, C])

                def step(ins):
                    n[0] += 1
                    ins.then_inc(lepe_done, 1)
                    pool.wait_ge(lepe_done, b * LEPE_OPS + n[0])

                pool.wait_ge(x_loaded, b * 16 + 16)
                pool.wait_ge(edges_loaded, b * 32 + 32)
                for k, tap in ((1, 1), (0, 0), (2, 2)):
                    step(combine(tmp, v_ext[:, k:k + T, :], row(tap), ALU.mult))
                    step(combine(base[:], base[:], tmp, ALU.add))
                step(combine(base[:], base[:], row(3), ALU.add))

            def add_attention(b_next):
                units.wait_read(pool, *b_next, ("O rows", -1))
                b = b_next[1]
                pool.wait_ge(out_stored, b * 16)
                combine(hres[:], attn[:], base[:], ALU.add).then_inc(sum_ready, 1)

            def ln_scales(m2, which):
                g = m2 + which
                pool.wait_ge(ln_stats, g * LN_OPS + LN_OPS)
                nc.gpsimd.tensor_tensor(neg_mean[:], moments[:, :, 0], ln_consts[:, :, 1], ALU.mult)
                nc.gpsimd.tensor_tensor(var_eps[:], moments[:, :, 1], ln_consts[:, :, 2], ALU.add)\
                    .then_inc(ln_scale, 1)
                pool.wait_ge(ln_scale, g * 3 + 1)
                nc.gpsimd.tensor_tensor(rstd[:], var_eps[:], ln_consts[:, :, 0], ALU.pow).then_inc(ln_scale, 1)
                pool.wait_ge(ln_scale, g * 3 + 2)
                nc.gpsimd.tensor_tensor(shift[:], neg_mean[:], rstd[:], ALU.mult).then_inc(ln_scale, 1)

            pool.dma_start(base[:], x[0]).then_inc(x_loaded, 16)
            nc.gpsimd.memset(neg_mean[:], 0.0).then_inc(out_stored, 16)
            nc.gpsimd.memset(v_pair[:], 0.0).then_inc(pool_setup, 1)
            nc.gpsimd.memset(ident[:], 0.0).then_inc(pool_setup, 1)
            for i, c in enumerate((-0.5, -1.0, EPS, 1.0)):
                nc.gpsimd.memset(ln_consts[:, :, i], c)
            nc.gpsimd.memset(v_ext[:, 0, :], 0.0)
            nc.gpsimd.memset(v_ext[:, T + 1, :], 0.0)
            pool.wait_ge(pool_setup, 2)
            nc.gpsimd.memset(v_pair[:, :, :, :, D:D + 1], 1.0).then_inc(pool_setup, 1)
            nc.gpsimd.affine_select(out=ident[:], in_=ident[:], compare_op=ALU.not_equal, fill=1.0, base=0,
                                    pattern=[[-1, P]], channel_multiplier=1).then_inc(pool_setup, 1)
            pool.wait_ge(weights_loaded, 9 * 16)
            rotate_and_split("start", 0, 0, 0)
            rotate_and_split("start", 0, 0, 1)

            def iteration(kind, b):
                if kind != "first":
                    add_attention((kind, b))
                    wait_apart(pool, sum_ready, b, (pool_setup, 4))
                    pool.dma_start(base[:], x[b]).then_inc(x_loaded, 16)
                lepe(b)
                if kind != "first":
                    ln_scales(b * 2 - 2, 0)
                if kind != "last":
                    rotate_and_split(kind, b, b + 1, 0)
                    rotate_and_split(kind, b, b + 1, 1)
                if kind != "first":
                    ln_scales(b * 2 - 2, 1)

            over_batches(pool, iteration)
            add_attention(("end", NB))
            ln_scales(2 * NB - 2, 0)
            ln_scales(2 * NB - 2, 1)


def kernel(**inputs):
    import concourse.bacc as bacc
    from concourse.bass_utils import run_bass_kernel_spmd

    x = np.asarray(inputs["L0_attn_x"])
    w_qkv = np.asarray(inputs["L0_attn_w_qkv"])
    b_qkv = np.asarray(inputs["L0_attn_b_qkv"])
    order = np.concatenate([which * C + c + 2 * np.arange(D // 2)[:, None] + D * np.arange(H)[None, :]
                            for which in range(2) for c in range(2)]).reshape(-1)
    rows = np.concatenate([order, 2 * C + np.arange(C)])
    xT = x.reshape(NB, P, T, KC, P).transpose(0, 4, 3, 2, 1).reshape(NB, P, KC, N)
    position = (T * np.arange(P)[None, :] + np.arange(T)[:, None]).reshape(1, N).astype(np.float32)
    freq = np.exp(np.arange(0, D, 2, dtype=np.float32) * np.float32(-np.log(10000.0) / D)).astype(np.float32)
    angle = np.repeat(freq, H)[:, None] * position
    arrays = {
        "x": x.reshape(NB, P, T, C),
        "xT": np.concatenate([xT, xT[:1]]),
        "wT": w_qkv[rows].T.reshape(KC, P, 3 * C).transpose(1, 0, 2),
        "b_qk": b_qkv[order].reshape(4, P).T,
        "b_v": b_qkv[2 * C:],
        "w_lepe": np.asarray(inputs["L0_attn_w_lepe"]).reshape(C, 3).T,
        "b_lepe": np.asarray(inputs["L0_attn_b_lepe"]),
        "cos": np.cos(angle),
        "sin": np.sin(angle),
        "k0": np.asarray(inputs["L0_ffn_k0"]),
        "k1": np.asarray(inputs["L0_ffn_k1"]),
        "k2": np.asarray(inputs["L0_ffn_k2"]),
        "s0": np.asarray(inputs["L0_ffn_s0"]).reshape(1),
        "s1": np.asarray(inputs["L0_ffn_s1"]).reshape(1),
        "s2": np.asarray(inputs["L0_ffn_s2"]).reshape(1),
    }
    nc = bacc.Bacc("TRN2", target_bir_lowering=False, num_devices=1)
    aps, fed = {}, {}
    for name, a in arrays.items():
        a = np.ascontiguousarray(a)
        fed[f"in_{name}"] = a
        aps[name] = nc.dram_tensor(f"in_{name}", list(a.shape), mybir.dt.from_np(a.dtype), kind="ExternalInput").ap()
    aps["out"] = nc.dram_tensor("out_0", [NB, P, T, C], F32, kind="ExternalOutput").ap()
    build(nc, **aps)
    r = run_bass_kernel_spmd(nc, [fed], core_ids=[0])
    return np.asarray(r.results[0]["out_0"]).reshape(NB, N, C)
```

```python
from contextlib import ExitStack

import numpy as np
import concourse.bass as bass
from concourse import mybir

ALU = mybir.AluOpType
ACT = mybir.ActivationFunctionType
AXIS_XY = mybir.AxisListType.XY
F32 = mybir.dt.float32
BF16 = mybir.dt.bfloat16
F16 = mybir.dt.float16
U8 = mybir.dt.uint8

P = 128
NB, N, C = 8, 1024, 256
H, D = 16, 16
F = 1024
T = N // P
KC = C // P
KF = F // P
PAIRS = H // 2
RING = 4
LEAD = 4
PARTS = 3
STACK = 6 * D
Q_PART = (0, 0, 0, 1, 1, 2)
K_PART = (0, 1, 2, 0, 1, 0)
EPS = 1e-5
H_SCALE = 2.0 ** 11
Y0_SCALE = 2.0 ** 6
Y1_SCALE = 2.0 ** -4
HI_PER_BATCH = 2 + 4 * T // 2
SPLIT_OPS = 14
START_OPS = (10, 14, 18, 22)
LEPE_OPS = 7
MAX_OPS = 4
LN_OPS = 2 * T
STATS_STEPS = ((6, 7, 11, 13, 14, 15, 19, 21), (35, 37, 38, 39, 43, 45, 46, 47))
NORMALISE_STEPS = (2 * T + 7, 6 * T + 1)
LOAD = 16 * 9


def b_units(kind):
    if kind == "first":
        return [("V", 0), ("V", 1)]
    ffn, proj = kind != "start", kind not in ("last", "end")
    l0 = lambda th: [("L0", th, u) for u in range(4)]
    l1 = lambda th: [("L1", th, u) for u in range(4)]
    order = [("hT", 0), ("hT", 1), ("proj", 0), ("proj", 1), *l0(0), *l1(0), ("proj", 2), ("proj", 3),
             *l0(1), ("L2", 0), *l1(1), ("V", 0), ("V", 1), ("L2", 1)]
    return [u for u in order if (proj if u[0] in ("proj", "V") else ffn)]


EARLY_PAIR = 1
EARLY_UNITS = [("proj", ct) for ct in range(4)]


def has_scores(kind, j, kt):
    return kind != "last" or (j + 1) * T + kt + LEAD < PAIRS * T


def has_max_rows(kind, j):
    return kind != "last" or j < PAIRS - 1


def o_rows_pair(kind, j, kt):
    if kt == 2 and j != PAIRS // 2 and not (j == 0 and kind == "first"):
        return j - 1
    return None


def plan_units(kind):
    def attention(units):
        double, single = [(0, 1), (2, 3)], [(4,), (5,), (6,)]
        used = {2: 0, 1: 0}
        for u in units:
            n = 2 if u[0] == "S" else 1
            ring = double if n == 2 else single
            yield u, ring[used[n] % len(ring)]
            used[n] += 1

    def stage_b(extra=(), which=None):
        n = 0
        for i, u in enumerate(which or b_units(kind)):
            yield u, ((0, 1), (2, 3), (4, 5))[n % 3]
            n += 1
            if i == 1:
                yield from ((x, (6,)) for x in extra)

    if kind == "start":
        scores = [("S", -1, v, h) for v in range(T + LEAD) for h in range(2)]
        scores.insert(2 * (T + 1), ("max rows", -1))
        return [*stage_b(), *attention(scores)]
    if kind == "end":
        return [(("O rows", -1), (6,)), *stage_b()]
    units = []
    for first in (0, PAIRS // 2):
        order = []
        if first:
            units += stage_b([("O rows", first - 1)])
        for j in range(first, first + PAIRS // 2):
            if kind == "first" and j == EARLY_PAIR:
                units += attention(order)
                units += stage_b(which=EARLY_UNITS)
                order = []
            for kt in range(T):
                for h in range(2):
                    if has_scores(kind, j, kt):
                        order.append(("S", j, kt, h))
                    if h == 1 and o_rows_pair(kind, j, kt) is not None:
                        order.append(("O rows", j - 1))
                    if h == 1 and kt == 5 and has_max_rows(kind, j):
                        order.append(("max rows", j))
                    order += [("T", j, kt, h, half) for half in range(2)]
        units += attention(order)
    return units


READERS = {"S": ("dve", "dve"), "T": ("act", "act"), "proj": ("act", "act"), "hT": ("act", "dve"),
           "L0": ("act", "dve"), "L1": ("act", "dve"), "L2": ("dve", "dve"), "V": ("dve", "dve"),
           "O rows": ("dve", "dve"), "max rows": ("dve", "dve")}


class Units:

    BANKS = 7

    def __init__(self, psum, full, free):
        self.psum, self.full, self.free = psum, full, free
        self.bank, self.nth, self.before, self.total = {}, {}, {}, {}
        left = {}
        for kind, previous in (("start", None), ("first", "start"), ("mid", "first"), ("last", "mid"),
                               ("end", "last")):
            count = dict.fromkeys([("full", "act"), ("full", "dve"), ("free", "act"), ("free", "dve")], 0)
            user = dict(left.get(previous, {}))
            waited = {"act": -NB * N, "dve": -NB * N}
            for u, banks in plan_units(kind):
                first, last = READERS[u[0]]
                need = {}
                for e, n in (user[k] for k in banks if k in user):
                    if n > waited[e]:
                        need[e] = waited[e] = n
                count["full", first] += 1
                count["free", last] += 1
                self.bank[kind, u], self.before[kind, u] = banks, need
                self.nth[kind, u] = (count["full", first], count["free", last])
                for k in banks:
                    user[k] = (last, count["free", last])
            self.total[kind] = count
            left[kind] = {k: (e, n - count["free", e]) for k, (e, n) in user.items()}
        assert left["first"] == left["mid"]

    def count(self, kind, b, which, n):
        t = {k: v[which] for k, v in self.total.items()}
        if kind == "start":
            return n
        n += t["start"]
        if kind == "first":
            return n
        n += t["first"]
        if kind == "mid":
            return b * t["mid"] + (n - t["mid"])
        n += (NB - 2) * t["mid"]
        return n if kind == "last" else n + t["last"]

    def half(self, kind, unit, i):
        return self.psum[:, self.bank[kind, unit][i], :]

    def both(self, kind, unit):
        lo, hi = self.bank[kind, unit]
        return self.psum[:, lo:hi + 1, :]

    def full_sem(self, unit):
        return self.full[READERS[unit[0]][0]]

    def free_sem(self, unit):
        return self.free[READERS[unit[0]][1]]

    def wait_free(self, eng, kind, b, unit, source=None):
        need = dict(self.before[kind, unit])
        if source is not None:
            e = READERS[source[0]][1]
            need[e] = max(need.get(e, 0), self.nth[kind, source][1])
        for e, n in need.items():
            wait(eng, self.free[e], self.count(kind, b, ("free", e), n))

    def wait_full(self, eng, kind, b, unit):
        e = READERS[unit[0]][0]
        wait(eng, self.full[e], self.count(kind, b, ("full", e), self.nth[kind, unit][0]))

    def wait_read(self, eng, kind, b, unit):
        e = READERS[unit[0]][1]
        wait(eng, self.free[e], self.count(kind, b, ("free", e), self.nth[kind, unit][1]))

    def wait_previous_read(self, eng, kind, b, e):
        wait(eng, self.free[e], self.count(kind, b, ("free", e), 0))


def wait(eng, sem, value):
    if isinstance(value, int) and value <= 0:
        return
    eng.wait_ge(sem, value)


def wait_apart(eng, sem, value, long_over):
    if not isinstance(value, int):
        value = eng.to_reg(value)
    eng.wait_ge(*long_over)
    eng.wait_ge(sem, value)


def over_batches(eng, iteration):
    iteration("first", 0)
    with eng.Fori(1, NB - 1) as b:
        iteration("mid", b)
    iteration("last", NB - 1)


def build(nc, x, xT, wT, b_qk, b_v, w_lepe, b_lepe, cos, sin, k0, k1, k2, s0, s1, s2, out):
    with ExitStack() as ctx:
        def sb(name, shape, dt):
            return ctx.enter_context(nc.sbuf_tensor(name, shape, dt))

        def sem(name):
            return ctx.enter_context(nc.semaphore(name))

        q_scratch = nc.dram_tensor("q_scratch", [NB, PARTS, 2, P, N], BF16)
        k_scratch = nc.dram_tensor("k_scratch", [NB, PARTS, 2, P, N], BF16)

        q_stack = sb("q_stack", [P, RING, 2 * N], BF16)
        k_stack = sb("k_stack", [P, RING, 2 * N], BF16)
        v_pair = sb("v_pair", [P, RING, T, 2, 32], F32)
        v_ext = sb("v_ext", [P, T + 2, C], F32)
        xT_sb = sb("xT_sb", [P, KC, N], F32)
        base = sb("base", [P, T, C], F32)
        attn = sb("attn", [P, T, C], F32)
        hres = sb("hres", [P, T, C], F32)
        probs = sb("probs", [P, 4, N], F32)
        wT_sb = sb("wT_sb", [P, KC, 3 * C], F32)
        w0 = sb("w0", [P, KC, F], F16)
        w1 = sb("w1", [P, KF, F], F16)
        w2 = sb("w2", [P, KF, C], F16)
        rope = sb("rope", [P, 2, N], F32)
        cos_sb, sin_sb = rope[:, 0], rope[:, 1]
        work = sb("work", [P, 4, N], F32)
        parts = sb("parts", [P, PARTS, N], BF16)
        hT = sb("hT", [P, 2, KC, N], F16)
        h0T = sb("h0T", [P, 2, KF, N // 2], F16)
        h1T = sb("h1T", [P, 2, KF, N // 2], F16)
        o_sb = sb("o_sb", [P, 512], F32)
        lepe_rows = sb("lepe_rows", [P, 5, C], F32)
        ident = sb("ident", [P, P], F32)
        ident16 = sb("ident16", [P, P], BF16)
        bias_qk = sb("bias_qk", [P, 4], F32)
        maxima = sb("maxima", [P, 2, 2 * T], F32)
        max_rest = sb("max_rest", [P, 2 * T], F32)
        max_parts = sb("max_parts", [P, P], BF16)
        max_rows = sb("max_rows", [P, P], BF16)
        rden = sb("rden", [P, 2 * T], F32)
        stats = sb("stats", [P, T, 6], F32)
        moments = sb("moments", [P, T, 2], F32)
        var_eps = sb("var_eps", [P, T], F32)
        neg_mean = sb("neg_mean", [P, T], F32)
        ln_consts = sb("ln_consts", [P, T, 4], F32)
        rstd = sb("rstd", [P, T], F32)
        shift = sb("shift", [P, T], F32)
        s_in = sb("s_in", [P, 3], F32)
        s_sign = sb("s_sign", [P, 3], F32)
        s_work = sb("s_work", [P, 6], F32)
        out_scale = s_work[:, 5:6]
        stage0 = hres[:].rearrange("p t c -> p (t c)").bitcast(U8)
        stage1 = attn[:].rearrange("p t c -> p (t c)").bitcast(U8)
        work_k = h1T[:].rearrange("p a k n -> p (a k n)").bitcast(F32).rearrange("p (a n) -> p a n", n=N)
        parts_b = hT[:].rearrange("p a k n -> p (a k n)").bitcast(BF16)[:, 0:PARTS * N]\
            .rearrange("p (a n) -> p a n", n=N)

        def work_of(kind, which):
            return work_k if which == 1 and kind in ("start", "first") else work[:]
        k0_u8 = stage0[:, 0:2 * KC * F].rearrange("p (k n) -> p k n", n=F)
        k2_u8 = stage0[:, 2 * KC * F:2 * KC * F + KF * C].rearrange("p (k n) -> p k n", n=C)
        k1_u8 = stage1[:, 0:KF * F].rearrange("p (k n) -> p k n", n=F)

        unit_banks = ctx.enter_context(nc.psum_tensor("unit_banks", [P, Units.BANKS, 512], F32))
        o_bank = ctx.enter_context(nc.psum_tensor("o_bank", [P, 512], F32))

        unit_full = {e: sem(f"unit_full_for_{e}") for e in ("act", "dve")}
        unit_free = {e: sem(f"unit_read_by_{e}") for e in ("act", "dve")}
        w_q_loaded = sem("w_q_loaded")
        w_kv_loaded = sem("w_kv_loaded")
        bias_loaded = sem("bias_loaded")
        rows_loaded = sem("rows_loaded")
        start_rotated = sem("start_rotated")
        start_split = sem("start_split")
        start_written = [sem(f"start_written_{i}") for i in range(2)]
        k_loaded = sem("k_loaded")
        xT_loaded = sem("xT_loaded")
        x_loaded = sem("x_loaded")
        stack_loaded = [sem(f"stack_loaded{i}") for i in range(RING)]
        max_loaded = sem("max_loaded")
        edges_loaded = sem("edges_loaded")
        scratch_written = sem("scratch_written")
        out_stored = sem("out_stored")
        pool_setup = sem("pool_setup")
        dve_setup = sem("dve_setup")
        weights_ready = sem("weights_ready")
        max_split = sem("max_split")
        pv_done = sem("pv_done")
        o_copied = sem("o_copied")
        v_copied = sem("v_copied")
        reciprocal_done = sem("reciprocal_done")
        attn_written = sem("attn_written")
        sum_ready = sem("sum_ready")
        lepe_done = sem("lepe_done")
        elu_done = sem("elu_done")
        split_done = sem("split_done")
        ln_stats = sem("ln_stats")
        ln_scale = sem("ln_scale")
        ln_done = sem("ln_done")
        hi_ready = sem("hi_ready")
        units = Units(unit_banks, unit_full, unit_free)

        block = ctx.enter_context(nc.Block())

        q_rows = q_scratch.ap().rearrange("b t c (i h) n -> b (t c i) (h n)", h=H)
        k_rows = k_scratch.ap().rearrange("b t c (i h) n -> b (t c i) (h n)", h=H)

        def rotate(combine, w, step):
            step(combine(w[:, 1], w[:, 2], sin_sb, ALU.mult))
            step(combine(w[:, 3], w[:, 0], cos_sb, ALU.mult))
            step(combine(w[:, 3], w[:, 3], w[:, 1], ALU.subtract))
            step(combine(w[:, 1], w[:, 0], sin_sb, ALU.mult))
            step(combine(w[:, 2], w[:, 2], cos_sb, ALU.mult))
            step(combine(w[:, 1], w[:, 1], w[:, 2], ALU.add))

        @block.sync
        def _(sp):
            def load_stacks(b, j):
                r = j % RING
                cols = slice(j * 2 * N, (j + 1) * 2 * N)
                for blk, part in enumerate(Q_PART):
                    sp.dma_start(q_stack[blk * D:(blk + 1) * D, r], q_rows[b, part * D:(part + 1) * D, cols])\
                      .then_inc(stack_loaded[r], 16)
                for blk, n in ((0, 3), (3, 2), (5, 1)):
                    sp.dma_start(k_stack[blk * D:(blk + n) * D, r], k_rows[b, 0:n * D, cols])\
                      .then_inc(stack_loaded[r], 16)

            def load_max(kind, b, j):
                units.wait_read(sp, kind, b, ("max rows", j))
                for p in range(PARTS):
                    sp.dma_start(q_stack[STACK + p:STACK + p + 1, (j + 1) % RING].rearrange("o (r q) -> o r q", q=P),
                                 max_rows[p * 2 * T:(p + 1) * 2 * T, :]).then_inc(max_loaded, 16)

            def load_edges(kind, b):
                units.wait_read(sp, kind, b, ("V", 1))
                sp.dma_start(v_ext[1:P, 0, :], v_ext[0:P - 1, T, :]).then_inc(edges_loaded, 16)
                sp.dma_start(v_ext[0:P - 1, T + 1, :], v_ext[1:P, 1, :]).then_inc(edges_loaded, 16)

            def store_out(m):
                sp.wait_ge(ln_done, (m * 2 + 2) * T)
                sp.dma_start(out[m], hres[:]).then_inc(out_stored, 16)

            sp.dma_start(wT_sb[:, :, 0:2 * P], wT[:, :, 0:2 * P]).then_inc(w_q_loaded, 16)
            sp.dma_start(xT_sb[:], xT[0]).then_inc(xT_loaded, 16)
            sp.dma_start(bias_qk[:], b_qk).then_inc(bias_loaded, 16)
            sp.dma_start(wT_sb[:, :, 2 * P:], wT[:, :, 2 * P:]).then_inc(w_kv_loaded, 16)
            sp.dma_start(rope[:, 0], cos).then_inc(rows_loaded, 16)
            sp.dma_start(rope[:, 1], sin).then_inc(rows_loaded, 16)
            for i in range(3):
                sp.dma_start(lepe_rows[:, i], w_lepe[i].partition_broadcast(P)).then_inc(rows_loaded, 16)
            sp.dma_start(lepe_rows[:, 3], b_lepe.partition_broadcast(P)).then_inc(rows_loaded, 16)
            sp.dma_start(lepe_rows[:, 4], b_v.partition_broadcast(P)).then_inc(rows_loaded, 16)
            for i, s in enumerate((s0, s1, s2)):
                sp.dma_start(s_in[:, i:i + 1], s.partition_broadcast(P)).then_inc(k_loaded, 16)
            sp.dma_start(k0_u8, k0.rearrange("(k p) n -> p k n", p=P)).then_inc(k_loaded, 16)
            sp.dma_start(k1_u8, k1.rearrange("(k p) n -> p k n", p=P)).then_inc(k_loaded, 16)
            sp.dma_start(k2_u8, k2.rearrange("(k p) n -> p k n", p=P)).then_inc(k_loaded, 16)
            units.wait_full(sp, "start", 0, ("V", 1))
            sp.dma_start(xT_sb[:], xT[1]).then_inc(xT_loaded, 16)
            for i in range(4):
                sp.wait_ge(start_split, START_OPS[i])
                sp.dma_start((q_scratch, k_scratch)[i // 2].ap()[0, :, i % 2].rearrange("t p n -> p t n"),
                             (parts[:], parts_b)[i % 2]).then_inc(start_written[i % 2], 16)
            for i in range(2):
                sp.wait_ge(start_written[i], 2 * 16)
            load_stacks(0, 0)
            load_stacks(0, 1)
            load_edges("start", 0)
            load_max("start", 0, -1)
            load_stacks(0, 2)
            load_stacks(0, 3)

            def iteration(kind, b):
                for j in range(PAIRS):
                    if j == PAIRS // 2 and kind != "last":
                        load_edges(kind, b)
                        if kind == "first":
                            units.wait_full(sp, kind, b, ("V", 1))
                            sp.dma_start(xT_sb[:], xT[2]).then_inc(xT_loaded, 16)
                        else:
                            units.wait_full(sp, kind, b, ("V", 1))
                            sp.dma_start(xT_sb[:], xT[b + 2]).then_inc(xT_loaded, 16)
                    if kind != "last" or j < PAIRS - 1:
                        load_max(kind, b, j)
                    if j == PAIRS - 1 and kind != "first":
                        store_out(b - 1)
                    if kind == "last" and j + RING >= PAIRS:
                        continue
                    units.wait_full(sp, kind, b, ("T", j, T - 1, 1, 1))
                    if j + RING < PAIRS:
                        load_stacks(b, j + RING)
                    else:
                        sp.wait_ge(scratch_written, b * 64 + 64)
                        load_stacks(b + 1, j + RING - PAIRS)

            over_batches(sp, iteration)
            store_out(NB - 1)
            sp.wait_ge(out_stored, 16 * (NB + 1))

        @block.tensor
        def _(pe):
            def scores(kind, b, unit, j, t, h):
                r = j % RING
                units.wait_free(pe, kind, b, unit)
                for half in range(2):
                    last = nc.tensor.matmul(units.half(kind, unit, half),
                                            q_stack[0:STACK, r, h * N + t * P:h * N + (t + 1) * P],
                                            k_stack[0:STACK, r, h * N + half * 512:h * N + (half + 1) * 512],
                                            start=True, stop=True)
                last.then_inc(units.full_sem(unit), 1)

            def scores_T(kind, b, j, kt, h):
                r, rows = j % RING, STACK + PARTS
                for half in range(2):
                    unit = ("T", j, kt, h, half)
                    units.wait_free(pe, kind, b, unit)
                    nc.tensor.matmul(units.half(kind, unit, 0),
                                     k_stack[0:rows, r, h * N + kt * P:h * N + (kt + 1) * P],
                                     q_stack[0:rows, r, h * N + half * 512:h * N + (half + 1) * 512],
                                     start=True, stop=True).then_inc(units.full_sem(unit), 1)

            def weighted_v(kind, b, j, kt):
                if kt == 0:
                    wait(pe, v_copied, b * PAIRS + (j + 1))
                    wait(pe, o_copied, b * PAIRS + j)
                if j < 0:
                    units.wait_previous_read(pe, kind, b, "act")
                else:
                    units.wait_read(pe, kind, b, ("T", j, kt, 1, 1))
                for parity in range(2):
                    for h in range(2):
                        g = 2 * parity + h
                        p = probs[:, 2 * (kt % 2) + h].rearrange("p (b f q) -> p b f q", f=2, q=P)
                        o = o_bank[32 * g:32 * g + 32, :].rearrange("p (b q) -> p b q", q=P)
                        last = nc.tensor.matmul(o, v_pair[:, j % RING, kt, h, :], p[:, :, parity, :],
                                                start=kt == 0, stop=kt == T - 1, skip_group_check=True)
                last.then_inc(pv_done, 1)

            def max_rows_T(kind, b, j):
                unit = ("max rows", j)
                wait(pe, max_split, b * (PAIRS * MAX_OPS) + (j + 2) * MAX_OPS)
                units.wait_free(pe, kind, b, unit)
                nc.tensor.transpose(units.half(kind, unit, 0).bitcast(BF16)[:, 0:P], max_parts[:], ident16[:])\
                  .then_inc(units.full_sem(unit), 1)

            def o_rows(kind, b, j):
                unit = ("O rows", j)
                pe.wait_ge(o_copied, b * PAIRS + (j + 1))
                units.wait_free(pe, kind, b, unit)
                for blk in range(4):
                    last = nc.tensor.transpose(units.half(kind, unit, 0)[:, blk * P:(blk + 1) * P],
                                               o_sb[:, blk * P:(blk + 1) * P], ident[:])
                last.then_inc(units.full_sem(unit), 1)

            def project(kind, b, ct):
                unit = ("proj", ct)
                units.wait_free(pe, kind, b, unit)
                for half in range(2):
                    for kc in range(KC):
                        last = nc.tensor.matmul(units.half(kind, unit, half),
                                                wT_sb[:, kc, ct * P:(ct + 1) * P],
                                                xT_sb[:, kc, half * 512:(half + 1) * 512],
                                                start=kc == 0, stop=kc == KC - 1)
                last.then_inc(units.full_sem(unit), 1)

            def project_v(kind, b, half):
                unit = ("V", half)
                units.wait_free(pe, kind, b, unit)
                for t in range(4):
                    for kc in range(KC):
                        col = (4 * half + t) * P
                        last = nc.tensor.matmul(units.half(kind, unit, t // 2)[:, t % 2 * C:(t % 2 + 1) * C], xT_sb[:, kc, col:col + P],
                                                wT_sb[:, kc, 2 * C:3 * C], start=kc == 0, stop=kc == KC - 1)
                last.then_inc(units.full_sem(unit), 1)

            def transpose_h(kind, b, kc):
                unit = ("hT", kc)
                units.wait_free(pe, kind, b, unit)
                for t in range(T):
                    last = nc.tensor.transpose(units.half(kind, unit, t // 4)[:, t % 4 * P:(t % 4 + 1) * P], hres[:, t, kc * P:(kc + 1) * P], ident[:])
                last.then_inc(units.full_sem(unit), 1)

            def hidden(kind, b, layer, th, u):
                unit = (layer, th, u)
                tiles = KC if layer == "L0" else KF
                for k in range(tiles):
                    source = ("hT", 1) if layer == "L0" else ("L0", th, k // 2)
                    if k == 0:
                        units.wait_free(pe, kind, b, unit, source)
                    elif layer == "L1" and k % 2 == 0:
                        units.wait_read(pe, kind, b, source)
                    for i in range(2):
                        m = (2 * u + i) * P
                        for part in range(2):
                            if layer == "L0":
                                w, a = w0[:, k, m:m + P], hT[:, part, k, th * 512:(th + 1) * 512]
                            else:
                                w, a = w1[:, k, m:m + P], h0T[:, part, k, :]
                            last = nc.tensor.matmul(units.half(kind, unit, i), w, a,
                                                    start=k == 0 and part == 0,
                                                    stop=k == tiles - 1 and part == 1)
                last.then_inc(units.full_sem(unit), 1)

            def ffn_out(kind, b, th):
                unit = ("L2", th)
                units.wait_free(pe, kind, b, unit, ("L1", th, 3))
                for t in range(4):
                    for k in range(KF):
                        for part in range(2):
                            last = nc.tensor.matmul(units.half(kind, unit, t // 2)[:, t % 2 * C:(t % 2 + 1) * C],
                                                    h1T[:, part, k, t * P:(t + 1) * P],
                                                    w2[:, k, :], start=k == 0 and part == 0,
                                                    stop=k == KF - 1 and part == 1)
                last.then_inc(units.full_sem(unit), 1)

            def stage_b(kind, b, after_unit, which=None):
                for n, unit in enumerate(which or b_units(kind)):
                    if unit == ("hT", 0):
                        pe.wait_ge(ln_done, b * (2 * T) - T)
                    if unit == ("proj", 0):
                        pe.wait_ge(xT_loaded, b * 16 + 32 if kind != "start" else 16)
                    if unit == ("proj", 2) and kind == "start":
                        pe.wait_ge(w_kv_loaded, 16)
                    if unit[0] == "proj":
                        project(kind, b, unit[1])
                    elif unit[0] == "V":
                        project_v(kind, b, unit[1])
                    elif unit[0] == "hT":
                        transpose_h(kind, b, unit[1])
                    elif unit[0] == "L2":
                        ffn_out(kind, b, unit[1])
                    else:
                        hidden(kind, b, *unit)
                    if n in after_unit:
                        after_unit[n]()

            def stack_uses(b, j):
                return (b * (PAIRS // RING) + (j // RING + 1)) * LOAD

            pe.wait_ge(w_q_loaded, 16)
            stage_b("start", 0, {})
            for v in range(T + LEAD):
                j = v // T
                if v % T == 0:
                    pe.wait_ge(stack_loaded[j], stack_uses(0, j))
                if v == T + 1:
                    pe.wait_ge(dve_setup, 2)
                    max_rows_T("start", 0, -1)
                for h in range(2):
                    scores("start", 0, ("S", -1, v, h), j, v % T, h)
            pe.wait_ge(pool_setup, 5)

            def iteration(kind, b):
                for j in range(PAIRS):
                    if kind == "first" and j == EARLY_PAIR:
                        stage_b(kind, b, {}, EARLY_UNITS)
                    if j == PAIRS // 2:
                        stage_b(kind, b, {0: lambda: weighted_v(kind, b, j - 1, T - 1),
                                          1: lambda: o_rows(kind, b, j - 1)})
                    for kt in range(T):
                        ahead = j * T + kt + T + LEAD
                        if kt == 0:
                            pe.wait_ge(max_loaded, b * (PAIRS * 48) + (j + 1) * 48)
                        if ahead % T == 0 and has_scores(kind, j, kt):
                            n = ahead // T
                            pe.wait_ge(stack_loaded[n % RING], stack_uses(b, n))
                        for h in range(2):
                            if has_scores(kind, j, kt):
                                scores(kind, b, ("S", j, kt, h), ahead // T, ahead % T, h)
                            if h == 1 and o_rows_pair(kind, j, kt) is not None:
                                o_rows(kind, b, j - 1)
                            if h == 1 and kt == 5 and has_max_rows(kind, j):
                                max_rows_T(kind, b, j)
                            if h == 1 and kt > 0:
                                weighted_v(kind, b, j, kt - 1)
                            elif h == 1 and j != PAIRS // 2 and not (j == 0 and kind == "first"):
                                weighted_v(kind, b, j - 1, T - 1)
                            scores_T(kind, b, j, kt, h)

            over_batches(pe, iteration)
            weighted_v("end", NB, -1, T - 1)
            o_rows("end", NB, -1)
            stage_b("end", NB, {})

        @block.scalar
        def _(act):
            def exp_probs(kind, b, j, kt, h, half):
                unit = ("T", j, kt, h, half)
                units.wait_full(act, kind, b, unit)
                if h == 0 and half == 0:
                    wait(act, pv_done, b * (PAIRS * T) + (j * T + kt - 1))
                nc.scalar.activation(probs[:, 2 * (kt % 2) + h, half * 512:(half + 1) * 512],
                                     units.half(kind, unit, 0), ACT.Exp, scale=float(D) ** -0.5)\
                  .then_inc(units.free_sem(unit), 1)

            def copy_o(kind, b, j):
                act.wait_ge(pv_done, b * (PAIRS * T) + (j + 1) * T)
                before = b * PAIRS + j
                if not (isinstance(before, int) and before == 0):
                    wait_o_rows(kind, b, j)
                nc.scalar.activation(o_sb[:], o_bank[:], ACT.Copy).then_inc(o_copied, 1)

            def wait_o_rows(kind, b, j):
                act.wait_ge(reciprocal_done, b * PAIRS + j)

            def copy_v(b, j):
                if not (isinstance(b, int) and b == 0 and j < RING):
                    act.wait_ge(pv_done, b * (PAIRS * T) + (j - RING + 1) * T)
                nc.scalar.activation(v_pair[:, j % RING, :, :, 0:D],
                                     v_ext[:, 1:T + 1, 2 * D * j:2 * D * (j + 1)]
                                     .rearrange("p t (h d) -> p t h d", d=D), ACT.Copy).then_inc(v_copied, 1)

            def next_v(kind, b, j):
                n = j + RING
                if n < PAIRS:
                    copy_v(b, n)
                elif kind != "last":
                    if j == RING:
                        units.wait_read(act, kind, b, ("V", 1))
                    copy_v(b + 1, n - PAIRS)

            def elu_inputs(kind, b, ct):
                unit = ("proj", ct)
                units.wait_full(act, kind, b, unit)
                if ct == 0 and kind != "start":
                    act.wait_ge(lepe_done, b * LEPE_OPS + LEPE_OPS)
                if ct % 2 == 0 and kind == "first":
                    act.wait_ge(start_split, START_OPS[-1])
                elif ct % 2 == 0 and kind == "mid":
                    act.wait_ge(split_done, b * (2 * SPLIT_OPS) + ct // 2 * SPLIT_OPS)
                for i, f in ((0, ACT.Exp), (1, ACT.Relu)):
                    last = nc.scalar.activation(work_of(kind, ct // 2)[:, 2 * (ct % 2) + i].rearrange("p (a n) -> p a n", a=2),
                                                units.both(kind, unit), f, bias=bias_qk[:, ct:ct + 1])
                last.then_inc(units.free_sem(unit), 1)

            def high_part(kind, b, unit):
                units.wait_full(act, kind, b, unit)
                s = units.both(kind, unit)
                if unit[0] == "hT":
                    ins = nc.scalar.activation(hT[:, 0, unit[1], :].rearrange("p (a n) -> p a n", a=2), s,
                                               ACT.Copy, scale=H_SCALE)
                else:
                    u = unit[2]
                    dst = h0T if unit[0] == "L0" else h1T
                    ins = nc.scalar.activation(dst[:, 0, 2 * u:2 * u + 2, :], s, ACT.Relu)
                ins.then_inc(hi_ready, 1)

            def stage_b(kind, b, after_unit, which=None):
                for n, unit in enumerate(which or b_units(kind)):
                    if unit[0] == "proj":
                        elu_inputs(kind, b, unit[1])
                    elif unit[0] in ("hT", "L0", "L1"):
                        high_part(kind, b, unit)
                    if n in after_unit:
                        after_unit[n]()

            def normalise(m2, which, t):
                if t == 0:
                    act.wait_ge(ln_scale, (m2 + which + 1) * 3)
                nc.scalar.activation(hres[:, t, :], hres[:, t, :], ACT.Identity, bias=shift[:, t:t + 1],
                                     scale=rstd[:, t:t + 1]).then_inc(ln_done, 1)

            act.wait_ge(bias_loaded, 16)
            stage_b("start", 0, {})
            act.wait_ge(pool_setup, 4)
            units.wait_read(act, "start", 0, ("V", 1))
            for j in range(RING):
                copy_v(0, j)

            def iteration(kind, b):
                for j in range(PAIRS):
                    if kind == "first" and j == EARLY_PAIR:
                        stage_b(kind, b, {}, EARLY_UNITS)
                    if j == PAIRS // 2:
                        stage_b(kind, b, {0: lambda: [copy_o(kind, b, j - 1), next_v(kind, b, j - 1)]})
                    for kt in range(T):
                        for h in range(2):
                            for half in range(2):
                                exp_probs(kind, b, j, kt, h, half)
                        if kt == 3 and j == 0 and kind != "first":
                            copy_v(b, RING - 1)
                        elif kt == 3 and j not in (0, PAIRS // 2):
                            next_v(kind, b, j - 1)
                        for which, start in enumerate(NORMALISE_STEPS):
                            if kind != "first" and 0 <= j * T + kt - start < T:
                                normalise(b * 2 - 2, which, j * T + kt - start)

            over_batches(act, iteration)
            copy_o("end", NB, -1)
            for t in range(T // 2):
                normalise(2 * NB - 2, 0, t)
            stage_b("end", NB, {})
            for t in range(T // 2):
                normalise(2 * NB - 2, 1, t)

        @block.vector
        def _(dve):
            def row_max(kind, b, unit, parity, t, h):
                units.wait_full(dve, kind, b, unit)
                nc.vector.reduce_max(maxima[:, parity, h * T + t:h * T + t + 1], units.both(kind, unit), AXIS_XY)\
                  .then_inc(units.free_sem(unit), 1)

            def split_max(kind, b, j, last_unit):
                units.wait_read(dve, kind, b, last_unit)
                n = b * (PAIRS * MAX_OPS) + (j + 1) * MAX_OPS
                m = maxima[:, (j + 1) % 2]
                part = [max_parts[:, i * 2 * T:(i + 1) * 2 * T] for i in range(PARTS)]
                nc.vector.tensor_scalar(part[0], m, -1.0, None, ALU.mult).then_inc(max_split, 1)
                dve.wait_ge(max_split, n + 1)
                nc.vector.scalar_tensor_tensor(max_rest[:], m, -1.0, part[0], ALU.mult, ALU.subtract)\
                  .then_inc(max_split, 1)
                dve.wait_ge(max_split, n + 2)
                nc.vector.tensor_copy(part[1], max_rest[:]).then_inc(max_split, 1)
                dve.wait_ge(max_split, n + 3)
                nc.vector.tensor_tensor(part[2], max_rest[:], part[1], ALU.subtract).then_inc(max_split, 1)

            def copy_max_rows(kind, b, j):
                unit = ("max rows", j)
                units.wait_full(dve, kind, b, unit)
                wait(dve, max_loaded, b * (PAIRS * 48) + (j + 1) * 48)
                nc.vector.tensor_copy(max_rows[:], units.half(kind, unit, 0).bitcast(BF16)[:, 0:P])\
                  .then_inc(units.free_sem(unit), 1)

            def normalise_o(kind, b, j, pair):
                unit = ("O rows", j)
                units.wait_full(dve, kind, b, unit)
                o = units.half(kind, unit, 0).rearrange("p (g c) -> p g c", c=32)
                nc.vector.reciprocal(rden[:], o[:, :, D]).then_inc(reciprocal_done, 1)
                dve.wait_ge(reciprocal_done, b * PAIRS + (j + 1))
                if pair == 0:
                    wait(dve, sum_ready, b)
                nc.vector.tensor_tensor(attn[:, :, 2 * D * pair:2 * D * (pair + 1)]
                                        .rearrange("p t (h d) -> p t h d", d=D),
                                        o[:, :, 0:D].rearrange("p (t h) d -> p t h d", h=2),
                                        rden[:].rearrange("p (t h) -> p t h", h=2).unsqueeze(3)
                                        .to_broadcast([P, T, 2, D]), ALU.mult)\
                  .then_inc(units.free_sem(unit), 1)

            def copy_o(b, j):
                dve.wait_ge(pv_done, b * (PAIRS * T) + (j + 1) * T)
                nc.vector.tensor_copy(o_sb[:], o_bank[:]).then_inc(o_copied, 1)

            def elu(kind, b, unit):
                units.wait_read(dve, kind, b, unit)
                w, c = work_of(kind, unit[1] // 2), 2 * (unit[1] % 2)
                nc.vector.scalar_tensor_tensor(w[:, c], w[:, c], 1.0, w[:, c + 1], ALU.min, ALU.add)\
                  .then_inc(elu_done, 1)

            def low_part(kind, b, unit, n):
                dve.wait_ge(hi_ready, b * HI_PER_BATCH + (n + 1 - HI_PER_BATCH))
                s = units.both(kind, unit)
                if unit[0] == "hT":
                    hi, lo = (hT[:, i, unit[1], :].rearrange("p (a n) -> p a n", a=2) for i in range(2))
                    ins = nc.vector.scalar_tensor_tensor(lo, s, H_SCALE, hi, ALU.mult, ALU.subtract)
                else:
                    u = unit[2]
                    dst = h0T if unit[0] == "L0" else h1T
                    ins = nc.vector.scalar_tensor_tensor(dst[:, 1, 2 * u:2 * u + 2, :],
                                                         s, 0.0, dst[:, 0, 2 * u:2 * u + 2, :], ALU.max, ALU.subtract)
                ins.then_inc(units.free_sem(unit), 1)

            def v_out(kind, b, half):
                unit = ("V", half)
                units.wait_full(dve, kind, b, unit)
                if half == 0 and kind != "start":
                    dve.wait_ge(v_copied, b * PAIRS + PAIRS)
                    dve.wait_ge(lepe_done, b * LEPE_OPS + LEPE_OPS)
                nc.vector.tensor_tensor(v_ext[:, 1 + 4 * half:5 + 4 * half, :].rearrange("p (a t) c -> p a t c", a=2),
                                        units.both(kind, unit).rearrange("p a (t c) -> p a t c", c=C),
                                        lepe_rows[:, 4:5].unsqueeze(1).to_broadcast([P, 2, 2, C]), ALU.add)\
                  .then_inc(units.free_sem(unit), 1)

            def ffn_residual(kind, b, th):
                unit = ("L2", th)
                units.wait_full(dve, kind, b, unit)
                h = hres[:, 4 * th:4 * th + 4, :].rearrange("p (a t) c -> p a t c", a=2)
                nc.vector.scalar_tensor_tensor(h, units.both(kind, unit).rearrange("p a (t c) -> p a t c", c=C),
                                               out_scale, h, ALU.mult, ALU.add).then_inc(units.free_sem(unit), 1)

            def stage_b(kind, b, after_unit, which=None):
                n = 0
                for i, unit in enumerate(which or b_units(kind)):
                    if unit[0] == "V":
                        v_out(kind, b, unit[1])
                    elif unit[0] == "L2":
                        ffn_residual(kind, b, unit[1])
                    elif unit[0] == "proj":
                        elu(kind, b, unit)
                    else:
                        low_part(kind, b, unit, n)
                        n += 1
                    if i in after_unit:
                        after_unit[i]()

            def ln_tile(m2, which, t):
                nc.vector.bn_stats(stats[:, t, :], hres[:, t, :]).then_inc(ln_stats, 1)
                if t == T - 1:
                    for i in range(T):
                        if i == 0:
                            wait_apart(dve, ln_stats, (m2 + which) * LN_OPS + T, (dve_setup, 2))
                        nc.vector.bn_aggr(moments[:, i, :], stats[:, i, :]).then_inc(ln_stats, 1)

            def split_start(which, src, tmp, dst, i):
                n = START_OPS[i] - 4
                if i >= 2:
                    dve.wait_ge(start_written[i % 2], 16)
                nc.vector.tensor_copy(dst[:, 0], src).then_inc(start_split, 1)
                dve.wait_ge(start_split, n + 1)
                nc.vector.tensor_tensor(tmp, src, dst[:, 0], ALU.subtract).then_inc(start_split, 1)
                dve.wait_ge(start_split, n + 2)
                nc.vector.tensor_copy(dst[:, 1], tmp).then_inc(start_split, 1)
                dve.wait_ge(start_split, n + 3)
                nc.vector.tensor_tensor(dst[:, 2], tmp, dst[:, 1], ALU.subtract).then_inc(start_split, 1)
                dve.wait_ge(start_split, n + 4)

            for ct in range(2):
                elu("start", 0, ("proj", ct))
            dve.wait_ge(rows_loaded, 7 * 16)
            dve.wait_ge(elu_done, 2)
            n = [0]

            def rotated(ins):
                n[0] += 1
                ins.then_inc(start_split, 1)
                if n[0] in (2, 4):
                    elu("start", 0, ("proj", 1 + n[0] // 2))
                dve.wait_ge(start_split, n[0])

            rotate(nc.vector.tensor_tensor, work[:], rotated)
            split_start(0, work[:, 3], work[:, 0], parts[:], 0)
            split_start(0, work[:, 1], work[:, 2], parts_b, 1)
            dve.wait_ge(start_rotated, 3)
            split_start(1, work_k[:, 3], work[:, 0], parts[:], 2)
            dve.wait_ge(start_rotated, 6)
            split_start(1, work_k[:, 1], work_k[:, 2], parts_b, 3)
            for half in range(2):
                v_out("start", 0, half)

            dve.wait_ge(pool_setup, 4)
            nc.vector.tensor_copy(ident16[:], ident[:]).then_inc(dve_setup, 1)
            nc.vector.memset(max_parts[:], 0.0).then_inc(dve_setup, 1)
            dve.wait_ge(dve_setup, 2)
            for v in range(T + LEAD):
                if v == T + 1:
                    copy_max_rows("start", 0, -1)
                for h in range(2):
                    row_max("start", 0, ("S", -1, v, h), v // T, v % T, h)
                if v == T - 1:
                    split_max("start", 0, -1, ("S", -1, v, 1))

            dve.wait_ge(k_loaded, 6 * 16)
            steps = [0]

            def then(ins):
                steps[0] += 1
                ins.then_inc(weights_ready, 1)
                dve.wait_ge(weights_ready, steps[0])

            then(nc.vector.tensor_scalar(s_sign[:], s_in[:], 0.0, 2.0, ALU.is_ge, ALU.mult))
            then(nc.vector.tensor_scalar(s_sign[:], s_sign[:], -1.0, None, ALU.add))
            then(nc.vector.tensor_scalar(s_work[:, 0:1], s_sign[:, 0:1], 2.0 * Y0_SCALE / H_SCALE, None, ALU.mult))
            then(nc.vector.tensor_scalar(s_work[:, 1:2], s_sign[:, 1:2], 2.0 * Y1_SCALE / Y0_SCALE, None, ALU.mult))
            then(nc.vector.tensor_scalar(s_work[:, 2:3], s_work[:, 1:2], -0.5, None, ALU.mult))
            then(nc.vector.tensor_tensor(s_work[:, 3:4], s_in[:, 0:1], s_sign[:, 0:1], ALU.mult))
            then(nc.vector.tensor_tensor(s_work[:, 4:5], s_in[:, 1:2], s_sign[:, 1:2], ALU.mult))
            then(nc.vector.tensor_tensor(s_work[:, 3:4], s_work[:, 3:4], s_work[:, 4:5], ALU.mult))
            then(nc.vector.scalar_tensor_tensor(out_scale, s_work[:, 3:4], 4.0 / Y1_SCALE, s_in[:, 2:3],
                                                ALU.mult, ALU.mult))

            def weights(i):
                if i == 0:
                    then(nc.vector.tensor_tensor(w0[:], k0_u8[:, 0:KC], k0_u8[:, KC:2 * KC], ALU.subtract))
                    then(nc.vector.tensor_scalar(w0[:], w0[:], s_work[:, 0:1], None, ALU.mult))
                elif i <= 4:
                    k = slice(2 * i - 2, 2 * i)
                    then(nc.vector.tensor_scalar(w1[:, k], k1_u8[:, k], s_work[:, 1:2], s_work[:, 2:3],
                                                 ALU.mult, ALU.add))
                else:
                    then(nc.vector.tensor_scalar(w2[:], k2_u8, 2.0, -1.0, ALU.mult, ALU.add))

            def iteration(kind, b):
                for j in range(PAIRS):
                    if kind == "first" and j == EARLY_PAIR:
                        stage_b(kind, b, {}, EARLY_UNITS)
                    if j == PAIRS // 2:
                        stage_b(kind, b, {1: lambda: normalise_o(kind, b, j - 1, j - 1)})
                    for kt in range(T):
                        ahead = j * T + kt + T + LEAD
                        if kt == 4 and has_max_rows(kind, j):
                            split_max(kind, b, j, ("S", j, 3, 1))
                        for h in range(2):
                            if has_scores(kind, j, kt):
                                row_max(kind, b, ("S", j, kt, h), (ahead // T) % 2, ahead % T, h)
                            if h == 1 and kt == 5 and has_max_rows(kind, j):
                                copy_max_rows(kind, b, j)
                            if h == 1 and kt == 0 and j == 0 and kind != "first":
                                copy_o(b, -1)
                            elif h == 1 and kt == 0 and j not in (0, PAIRS // 2):
                                copy_o(b, j - 1)
                            if h == 1 and kt == 2 and j == 0 and kind != "first":
                                normalise_o(kind, b, -1, PAIRS - 1)
                            elif h == 1 and kt == 2 and j not in (0, PAIRS // 2):
                                normalise_o(kind, b, j - 1, j - 1)
                        if kind == "first" and j == 0 and kt < 6:
                            weights(kt)
                        for which in range(2):
                            if kind != "first" and j * T + kt in STATS_STEPS[which]:
                                t = STATS_STEPS[which].index(j * T + kt)
                                if t == 0 and which == 0:
                                    dve.wait_ge(sum_ready, b)
                                elif t == 0:
                                    units.wait_read(dve, kind, b, ("L2", 1))
                                ln_tile(b * 2 - 2, which, t)

            over_batches(dve, iteration)
            normalise_o("end", NB, -1, PAIRS - 1)

            def tiles(half):
                return range(half * T // 2, (half + 1) * T // 2)

            def normalise(which):
                dve.wait_ge(ln_scale, (2 * NB - 2 + which + 1) * 3)
                for t in tiles(1):
                    nc.vector.tensor_scalar(hres[:, t, :], hres[:, t, :], rstd[:, t:t + 1], shift[:, t:t + 1],
                                            ALU.mult, ALU.add).then_inc(ln_done, 1)

            def stats_half(which, half):
                for t in tiles(half):
                    ln_tile(2 * NB - 2, which, t)

            units.wait_read(dve, "end", NB, ("O rows", -1))
            dve.wait_ge(lepe_done, NB * LEPE_OPS)
            dve.wait_ge(out_stored, NB * 16)
            for half in range(2):
                rows = slice(tiles(half).start, tiles(half).stop)
                nc.vector.tensor_tensor(hres[:, rows, :], attn[:, rows, :], base[:, rows, :], ALU.add)\
                  .then_inc(sum_ready, 1)
            for half in range(2):
                dve.wait_ge(sum_ready, NB + half)
                stats_half(0, half)
            normalise(0)

            def first_half():
                units.wait_read(dve, "end", NB, ("L2", 0))
                stats_half(1, 0)

            stage_b("end", NB, {b_units("end").index(("L1", 1, 3)): first_half})
            units.wait_read(dve, "end", NB, ("L2", 1))
            stats_half(1, 1)
            normalise(1)

        @block.gpsimd
        def _(pool):
            combine = nc.gpsimd.tensor_tensor

            def rotate_and_split(kind, b, batch, which):
                g = ((batch - 1) * 2 + which) * SPLIT_OPS
                pool.wait_ge(elu_done, batch * 4 + 2 * which + 2)
                w = work_of(kind, which)
                one = ln_consts[:, 0, 3:4].to_broadcast([P, N])
                n = [0]

                def step(ins, before_dma=False):
                    n[0] += 1
                    ins.then_inc(split_done, 1)
                    if before_dma:
                        wait_apart(pool, split_done, g + n[0], (pool_setup, 4))
                    else:
                        pool.wait_ge(split_done, g + n[0])

                rotate(combine, w, step)
                scratch = (q_scratch, k_scratch)[which]
                for c, (o, rest) in enumerate(((w[:, 3], w[:, 0]), (w[:, 1], w[:, 0]))):
                    sent = (((batch - 1) * 2 + which) * 2 + c) * 16
                    if not (isinstance(sent, int) and sent == 0):
                        pool.wait_ge(scratch_written, sent)
                    step(combine(parts[:, 0], o, one, ALU.mult))
                    step(combine(rest, o, parts[:, 0], ALU.subtract))
                    step(combine(parts[:, 1], rest, one, ALU.mult))
                    step(combine(parts[:, 2], rest, parts[:, 1], ALU.subtract), before_dma=True)
                    pool.dma_start(scratch.ap()[batch, :, c].rearrange("t p n -> p t n"), parts[:])\
                        .then_inc(scratch_written, 16)

            def lepe(b):
                n = [0]
                tmp = work[:, 0:2].rearrange("p a (t c) -> p (a t) c", c=C)
                row = lambda i: lepe_rows[:, i].unsqueeze(1).to_broadcast([P, T, C])

                def step(ins):
                    n[0] += 1
                    ins.then_inc(lepe_done, 1)
                    pool.wait_ge(lepe_done, b * LEPE_OPS + n[0])

                pool.wait_ge(x_loaded, b * 16 + 16)
                pool.wait_ge(edges_loaded, b * 32 + 32)
                for k, tap in ((1, 1), (0, 0), (2, 2)):
                    step(combine(tmp, v_ext[:, k:k + T, :], row(tap), ALU.mult))
                    step(combine(base[:], base[:], tmp, ALU.add))
                step(combine(base[:], base[:], row(3), ALU.add))

            def add_attention(kind, b):
                units.wait_read(pool, kind, b, ("O rows", -1))
                pool.wait_ge(out_stored, b * 16)
                combine(hres[:], attn[:], base[:], ALU.add).then_inc(sum_ready, 1)

            def ln_scales(m2, which):
                g = m2 + which
                pool.wait_ge(ln_stats, g * LN_OPS + LN_OPS)
                nc.gpsimd.tensor_tensor(neg_mean[:], moments[:, :, 0], ln_consts[:, :, 1], ALU.mult)
                nc.gpsimd.tensor_tensor(var_eps[:], moments[:, :, 1], ln_consts[:, :, 2], ALU.add)\
                    .then_inc(ln_scale, 1)
                pool.wait_ge(ln_scale, g * 3 + 1)
                nc.gpsimd.tensor_tensor(rstd[:], var_eps[:], ln_consts[:, :, 0], ALU.pow).then_inc(ln_scale, 1)
                pool.wait_ge(ln_scale, g * 3 + 2)
                nc.gpsimd.tensor_tensor(shift[:], neg_mean[:], rstd[:], ALU.mult).then_inc(ln_scale, 1)

            pool.dma_start(base[:], x[0]).then_inc(x_loaded, 16)
            nc.gpsimd.memset(neg_mean[:], 0.0).then_inc(out_stored, 16)
            nc.gpsimd.memset(v_pair[:], 0.0).then_inc(pool_setup, 1)
            nc.gpsimd.memset(ident[:], 0.0).then_inc(pool_setup, 1)
            for i, c in enumerate((-0.5, -1.0, EPS, 1.0)):
                nc.gpsimd.memset(ln_consts[:, :, i], c)
            nc.gpsimd.memset(v_ext[:, 0, :], 0.0)
            nc.gpsimd.memset(v_ext[:, T + 1, :], 0.0)
            pool.wait_ge(pool_setup, 2)
            nc.gpsimd.memset(v_pair[:, :, :, :, D:D + 1], 1.0).then_inc(pool_setup, 1)
            nc.gpsimd.affine_select(out=ident[:], in_=ident[:], compare_op=ALU.not_equal, fill=1.0, base=0,
                                    pattern=[[-1, P]], channel_multiplier=1).then_inc(pool_setup, 1)
            pool.wait_ge(pool_setup, 4)
            nc.gpsimd.memset(k_stack[STACK:P, :, :], 1.0).then_inc(pool_setup, 1)
            pool.wait_ge(pool_setup, 5)
            pool.wait_ge(rows_loaded, 7 * 16)
            pool.wait_ge(elu_done, 4)
            n = [0]

            def rotated(ins):
                n[0] += 1
                ins.then_inc(start_rotated, 1)
                pool.wait_ge(start_rotated, n[0])

            rotate(combine, work_k, rotated)

            def iteration(kind, b):
                if kind != "first":
                    add_attention(kind, b)
                    wait_apart(pool, sum_ready, b, (pool_setup, 4))
                    pool.dma_start(base[:], x[b]).then_inc(x_loaded, 16)
                lepe(b)
                if kind != "first":
                    ln_scales(b * 2 - 2, 0)
                if kind != "last":
                    rotate_and_split(kind, b, b + 1, 0)
                    rotate_and_split(kind, b, b + 1, 1)
                if kind != "first":
                    ln_scales(b * 2 - 2, 1)

            over_batches(pool, iteration)
            ln_scales(2 * NB - 2, 0)
            ln_scales(2 * NB - 2, 1)


def kernel(**inputs):
    import concourse.bacc as bacc
    from concourse.bass_utils import run_bass_kernel_spmd

    x = np.asarray(inputs["L0_attn_x"])
    w_qkv = np.asarray(inputs["L0_attn_w_qkv"])
    b_qkv = np.asarray(inputs["L0_attn_b_qkv"])
    order = np.concatenate([which * C + c + 2 * np.arange(D // 2)[:, None] + D * np.arange(H)[None, :]
                            for which in range(2) for c in range(2)]).reshape(-1)
    rows = np.concatenate([order, 2 * C + np.arange(C)])
    xT = x.reshape(NB, P, T, KC, P).transpose(0, 4, 3, 2, 1).reshape(NB, P, KC, N)
    position = (T * np.arange(P)[None, :] + np.arange(T)[:, None]).reshape(1, N).astype(np.float32)
    freq = np.exp(np.arange(0, D, 2, dtype=np.float32) * np.float32(-np.log(10000.0) / D)).astype(np.float32)
    angle = np.repeat(freq, H)[:, None] * position
    arrays = {
        "x": x.reshape(NB, P, T, C),
        "xT": np.concatenate([xT, xT[:1]]),
        "wT": w_qkv[rows].T.reshape(KC, P, 3 * C).transpose(1, 0, 2),
        "b_qk": b_qkv[order].reshape(4, P).T,
        "b_v": b_qkv[2 * C:],
        "w_lepe": np.asarray(inputs["L0_attn_w_lepe"]).reshape(C, 3).T,
        "b_lepe": np.asarray(inputs["L0_attn_b_lepe"]),
        "cos": np.cos(angle),
        "sin": np.sin(angle),
        "k0": np.asarray(inputs["L0_ffn_k0"]),
        "k1": np.asarray(inputs["L0_ffn_k1"]),
        "k2": np.asarray(inputs["L0_ffn_k2"]),
        "s0": np.asarray(inputs["L0_ffn_s0"]).reshape(1),
        "s1": np.asarray(inputs["L0_ffn_s1"]).reshape(1),
        "s2": np.asarray(inputs["L0_ffn_s2"]).reshape(1),
    }
    nc = bacc.Bacc("TRN2", target_bir_lowering=False, num_devices=1)
    aps, fed = {}, {}
    for name, a in arrays.items():
        a = np.ascontiguousarray(a)
        fed[f"in_{name}"] = a
        aps[name] = nc.dram_tensor(f"in_{name}", list(a.shape), mybir.dt.from_np(a.dtype), kind="ExternalInput").ap()
    aps["out"] = nc.dram_tensor("out_0", [NB, P, T, C], F32, kind="ExternalOutput").ap()
    build(nc, **aps)
    r = run_bass_kernel_spmd(nc, [fed], core_ids=[0])
    return np.asarray(r.results[0]["out_0"]).reshape(NB, N, C)
```
